# Optimizing a Trainium2 kernel written in Bass

```python
import numpy as np
import jax
import jax.numpy as jnp

def _softmax(x, axis=-1):
    return jax.nn.softmax(x, axis=axis)

def _gelu(x):
    return jax.nn.gelu(x, approximate=True)

def _silu(x):
    return jax.nn.silu(x)

def _sigmoid(x):
    return jax.nn.sigmoid(x)

def _layernorm(x, axis=-1, eps=1e-05):
    m = jnp.mean(x, axis=axis, keepdims=True)
    v = jnp.var(x, axis=axis, keepdims=True)
    return (x - m) / jnp.sqrt(v + eps)

def _scatter_add(tgt, idx, src, axis=0):
    return tgt.at[idx].add(src)

def _segment_sum(src, seg, n):
    return jax.ops.segment_sum(src, seg, n)
kernel_name = 'mk_cond_resid_d4_seqx_r4_ec006d'

def setup_inputs(seed: int=0):
    np.random.seed(seed)
    _w = jnp.asarray

    def _rec_inputs():
        import jax
        import jax.numpy as jnp
        _rk = jax.random.key(seed)
        x = -0.000125 + 0.9999 * jax.random.normal(jax.random.fold_in(_rk, 1), (2, 1024, 256), jnp.float32)
        _lenS = 1024 - jax.random.randint(jax.random.fold_in(_rk, 7), (2,), 0, max(1, 1024 // 4) + 1, jnp.int32)
        _lenS2 = 1024 - jax.random.randint(jax.random.fold_in(_rk, 8), (2,), 0, max(1, 1024 // 4) + 1, jnp.int32)
        cond_1024 = -0.00493535 + 1.00056 * jax.random.normal(jax.random.fold_in(_rk, 11), (2, 256), jnp.float32)
        return (x, cond_1024)
    x, cond_1024 = _rec_inputs()

    def _L0_cond_setup():
        import jax, jax.numpy as jnp
        import numpy as np
        import math
        N, T, D, H = (64, 128, 256, 256)
        key = jax.random.key(seed)
        k1, k2, k3, k4 = jax.random.split(key, 4)
        x = jax.random.normal(k1, (N, T, D), dtype=jnp.float32)
        h0 = jax.random.normal(k2, (N, H), dtype=jnp.float32)
        Wx = jax.random.normal(k3, (D, H), dtype=jnp.float32) / math.sqrt(D)
        Wh = jax.random.normal(k4, (H, H), dtype=jnp.float32) / math.sqrt(H)
        b = jnp.zeros((H,), dtype=jnp.float32)
        return {'x': x, 'h0': h0, 'Wx': Wx, 'Wh': Wh, 'b': b}
    _L0_cond_all = _L0_cond_setup()
    _L0_cond_in = {k: v for k, v in _L0_cond_all.items() if k in ('Wx', 'Wh', 'b')}
    del _L0_cond_all

    def _L1_cond_setup():
        import jax, jax.numpy as jnp
        import numpy as np
        D = 256
        H = 256
        key = jax.random.key(seed)
        k1, k2, k3, k4 = jax.random.split(key, 4)
        x = jax.random.normal(k1, (32, 128, D), dtype=jnp.float32)
        h0 = jax.random.normal(k2, (32, H), dtype=jnp.float32)
        Wx = jax.random.normal(k3, (D, 4 * H), dtype=jnp.float32) / jnp.sqrt(float(D))
        Wh = jax.random.normal(k4, (H, 4 * H), dtype=jnp.float32) / jnp.sqrt(float(H))
        b = jnp.zeros((4 * H,), dtype=jnp.float32)
        return {'x': x, 'h0': h0, 'Wx': Wx, 'Wh': Wh, 'b': b}
    _L1_cond_all = _L1_cond_setup()
    _L1_cond_in = {k: v for k, v in _L1_cond_all.items() if k in ('Wx', 'Wh', 'b')}
    del _L1_cond_all

    def _L2_cond_setup():
        import jax, jax.numpy as jnp
        import numpy as np
        N, T, D, H = (64, 128, 256, 256)
        key = jax.random.key(seed)
        k1, k2, k3, k4 = jax.random.split(key, 4)
        x = jax.random.normal(k1, (N, T, D), dtype=jnp.float32)
        h0 = jax.random.normal(k2, (N, H), dtype=jnp.float32)
        Wx = jax.random.normal(k3, (D, H), dtype=jnp.float32) / np.sqrt(D)
        Wh = jax.random.normal(k4, (H, H), dtype=jnp.float32) / np.sqrt(H)
        b = jnp.zeros((H,), dtype=jnp.float32)
        return {'x': x, 'h0': h0, 'Wx': Wx, 'Wh': Wh, 'b': b}
    _L2_cond_all = _L2_cond_setup()
    _L2_cond_in = {k: v for k, v in _L2_cond_all.items() if k in ('Wx', 'Wh', 'b')}
    del _L2_cond_all

    def _L3_cond_setup():
        import jax, jax.numpy as jnp
        import numpy as np
        import math
        N, T, D, H = (64, 128, 256, 256)
        key = jax.random.key(seed)
        k1, k2, k3, k4 = jax.random.split(key, 4)
        x = jax.random.normal(k1, (N, T, D), dtype=jnp.float32)
        h0 = jax.random.normal(k2, (N, H), dtype=jnp.float32)
        Wx = jax.random.normal(k3, (D, 4 * H), dtype=jnp.float32) / math.sqrt(D)
        Wh = jax.random.normal(k4, (H, 4 * H), dtype=jnp.float32) / math.sqrt(H)
        b = jnp.zeros((4 * H,), dtype=jnp.float32)
        return {'x': x, 'h0': h0, 'Wx': Wx, 'Wh': Wh, 'b': b}
    _L3_cond_all = _L3_cond_setup()
    _L3_cond_in = {k: v for k, v in _L3_cond_all.items() if k in ('Wx', 'Wh', 'b')}
    del _L3_cond_all
    return {'x': x, 'cond_1024': cond_1024, 'L0_cond_Wx': _L0_cond_in['Wx'], 'L0_cond_Wh': _L0_cond_in['Wh'], 'L0_cond_b': _L0_cond_in['b'], 'L1_cond_Wx': _L1_cond_in['Wx'], 'L1_cond_Wh': _L1_cond_in['Wh'], 'L1_cond_b': _L1_cond_in['b'], 'L2_cond_Wx': _L2_cond_in['Wx'], 'L2_cond_Wh': _L2_cond_in['Wh'], 'L2_cond_b': _L2_cond_in['b'], 'L3_cond_Wx': _L3_cond_in['Wx'], 'L3_cond_Wh': _L3_cond_in['Wh'], 'L3_cond_b': _L3_cond_in['b']}

def reference(x, cond_1024, L0_cond_Wx, L0_cond_Wh, L0_cond_b, L1_cond_Wx, L1_cond_Wh, L1_cond_b, L2_cond_Wx, L2_cond_Wh, L2_cond_b, L3_cond_Wx, L3_cond_Wh, L3_cond_b):
    import jax
    import jax.numpy as jnp

    def _L0_cond_ref(x, h0, Wx, Wh, b):
        import jax, jax.numpy as jnp
        import numpy as np
        import math
        N, T, D, H = (64, 128, 256, 256)
        xW = jnp.einsum('ntd,dh->nth', x, Wx) + b

        def step(prev_h, xw_t):
            next_h = jnp.tanh(prev_h @ Wh + xw_t)
            return (next_h, next_h)
        _, hs = jax.lax.scan(step, h0, jnp.swapaxes(xW, 0, 1))
        return jnp.swapaxes(hs, 0, 1)

    def _L1_cond_ref(x, h0, Wx, Wh, b):
        import jax, jax.numpy as jnp
        import numpy as np
        D = 256
        H = 256
        Hdim = h0.shape[1]
        x_proj = jnp.einsum('ntd,df->ntf', x, Wx) + b

        def step(carry, xp_t):
            prev_h, prev_c = carry
            h_bar = xp_t + prev_h @ Wh
            i = jax.nn.sigmoid(h_bar[:, 0:Hdim])
            f = jax.nn.sigmoid(h_bar[:, Hdim:2 * Hdim])
            o = jax.nn.sigmoid(h_bar[:, 2 * Hdim:3 * Hdim])
            g = jnp.tanh(h_bar[:, 3 * Hdim:4 * Hdim])
            next_c = f * prev_c + i * g
            next_h = o * jnp.tanh(next_c)
            return ((next_h, next_c), next_h)
        c0 = jnp.zeros_like(h0)
        xs = jnp.swapaxes(x_proj, 0, 1)
        _, hs = jax.lax.scan(step, (h0, c0), xs)
        return jnp.swapaxes(hs, 0, 1)

    def _L2_cond_ref(x, h0, Wx, Wh, b):
        import jax, jax.numpy as jnp
        import numpy as np
        N, T, D, H = (64, 128, 256, 256)
        xW = jnp.einsum('ntd,dh->nth', x, Wx) + b
        xW_t = jnp.swapaxes(xW, 0, 1)

        def step(prev_h, xw):
            next_h = jnp.tanh(prev_h @ Wh + xw)
            return (next_h, next_h)
        _, h_t = jax.lax.scan(step, h0, xW_t)
        return jnp.swapaxes(h_t, 0, 1)

    def _L3_cond_ref(x, h0, Wx, Wh, b):
        import jax, jax.numpy as jnp
        import numpy as np
        import math
        N, T, D, H = (64, 128, 256, 256)
        Hdim = h0.shape[1]
        xW = jnp.einsum('ntd,dg->ntg', x, Wx) + b

        def step(carry, xw_t):
            prev_h, prev_c = carry
            a = xw_t + prev_h @ Wh
            i = jax.nn.sigmoid(a[:, :Hdim])
            f = jax.nn.sigmoid(a[:, Hdim:2 * Hdim])
            o = jax.nn.sigmoid(a[:, 2 * Hdim:3 * Hdim])
            g = jnp.tanh(a[:, 3 * Hdim:])
            next_c = f * prev_c + i * g
            next_h = o * jnp.tanh(next_c)
            return ((next_h, next_c), next_h)
        c0 = jnp.zeros_like(h0)
        _, hs = jax.lax.scan(step, (h0, c0), jnp.swapaxes(xW, 0, 1))
        return jnp.swapaxes(hs, 0, 1)
    x = x + _L0_cond_ref(x, cond_1024, L0_cond_Wx, L0_cond_Wh, L0_cond_b)
    x = x + _L1_cond_ref(x, cond_1024, L1_cond_Wx, L1_cond_Wh, L1_cond_b)
    x = x + _L2_cond_ref(x, cond_1024, L2_cond_Wx, L2_cond_Wh, L2_cond_b)
    x = x + _L3_cond_ref(x, cond_1024, L3_cond_Wx, L3_cond_Wh, L3_cond_b)
    return x

_drawn_inputs = setup_inputs


def setup_inputs(seed=0):
    import zlib

    import numpy as np

    out = dict(_drawn_inputs(seed))
    spreads = {'L0_cond_b': (0.0, 0.1),
     'L1_cond_b': (0.0, 0.297),
     'L2_cond_b': (0.0, 0.1),
     'L3_cond_b': (0.0, 0.434)}
    factors = {}
    for name, (base, spread) in spreads.items():
        noise = np.random.default_rng([zlib.crc32(name.encode()), seed]).standard_normal(out[name].shape)
        drawn = base * np.exp(spread * noise) if base else spread * noise
        out[name] = jnp.asarray(drawn.astype(out[name].dtype))
    for name, factor in factors.items():
        out[name] = (out[name] * factor).astype(out[name].dtype)
    return out
```

```python
from contextlib import ExitStack

import numpy as np

import concourse.bass as bass
from concourse import mybir

F32 = mybir.dt.float32
F16 = mybir.dt.float16
BF16 = mybir.dt.bfloat16
I32 = mybir.dt.int32
ALU = mybir.AluOpType
TANH = mybir.ActivationFunctionType.Tanh
COPY = mybir.ActivationFunctionType.Copy
AX = mybir.AxisListType

P = 128
B, T, D = 2, 1024, 256
KT = D // P
CH = 16
NCH = T // CH
BODY = 2 * CH
NL = 4
IS_LSTM = [False, True, False, True]
LAG = [0, 28, 48, 76]
RNN_PHASE = LAG[0] % CH
LSTM_PHASE = LAG[1] % CH
STREAMS = [(0, 1), (2, 3)]
STEPS = LAG[3] + T
LOOP_FROM = 3 * BODY
LOOP_TO = T - BODY

HSCALE = 2.0 ** 14
TOP = 2.0 ** 14
LEAST_MAX = 2.0 ** -20
EXPONENT_BITS = 0x7F800000

GATES = [4 * KT if lstm else KT for lstm in IS_LSTM]
TILE0 = [0, GATES[0], GATES[0] + GATES[1], GATES[0] + GATES[1] + GATES[2]]
NT = sum(GATES)
CRIT = [0, 1, 2, 3, 6, 7]
OGATE = [4, 5]
RNN_TILES = [0, 1]
SIGMOID_COLS = 3 * D

BANK = 512
COLS = 2 * B
CRIT_STEP = len(CRIT) * COLS
REST_STEP = KT * COLS
CRIT_BANK = [[0, 1], [2, 3]]
O_BANK = [4, 6]
R_BANK = [7, 5]
REST_REGION = CH * REST_STEP


def bias_patterns():
    out = np.zeros((3, 32, NT, CH * B), np.float32)
    for tile in range(NT):
        out[:, tile, tile] = 1.0
    return out.reshape(96, -1)


def build(nc, x, cond, wx, wh, bias, pattern, half, out):
    ctx = ExitStack()
    with ctx:
        def sb(name, shape, dt=F32):
            return ctx.enter_context(nc.sbuf_tensor(name, shape, dt))

        def sem(name):
            return ctx.enter_context(nc.semaphore(name))

        wh_f = sb("wh_f", [P, KT, NT * P])
        wx_f = sb("wx_f", [P, KT, NT * P])
        wh_p = sb("wh_p", [P, 2, KT, NT * P], F16)
        cond_f = sb("cond_f", [P, KT, B])
        bias_f = sb("bias_f", [96, P])
        bias_r = sb("bias_r", [96, 2, P])
        bias_s = sb("bias_s", [96, 3, P], BF16)
        bias_p = sb("bias_p", [96, P], BF16)
        patt = sb("patt", [96, NT, CH * B], BF16)
        half_c = sb("half_c", [96, 1])
        largest = sb("largest", [P, 3])
        largest_all = sb("largest_all", [P, 3])
        power = sb("power", [P, 3])
        x_w = sb("x_w", [P, 1])
        total = sb("total", [P, 1])
        inv = sb("inv", [P, 2])
        wh_scale = sb("wh_scale", [P, 1])
        wx_scale = sb("wx_scale", [P, 1])
        b_scale = sb("b_scale", [P, 1])
        z_scale = sb("z_scale", [P, 1])
        up = sb("up", [P, KT * CH * B])
        down = sb("down", [P, KT * CH * B])
        xsplit = sb("xsplit", [P, KT, CH * B])
        x_all = sb("x_all", [P, T * KT * B])
        wx_p = sb("wx_p", [P, 2, KT, NT * P], F16)
        xtmp = [sb(f"xtmp{l}", [P, KT, CH * B]) for l in range(NL)]
        x_p = [sb(f"x_p{l}", [P, 2, KT, 2, CH * B], F16) for l in range(NL)]
        xs = [sb(f"x{l}", [P, 2, KT, CH * B]) for l in range(NL + 1)]
        x_out = sb("x_out", [P, 2, KT * CH * B])
        zr = [sb(f"zr{g}", [P, 2 * KT * B]) for g in range(2)]
        gates = [sb(f"gates{g}", [P, 16]) for g in range(2)]
        rest = [sb(f"rest{g}", [P, 12]) for g in range(2)]
        mult = [sb(f"mult{g}", [P, 8]) for g in range(2)]
        prod = [sb(f"prod{g}", [P, 8]) for g in range(2)]
        hist = [sb(f"hist{g}", [P, 2, BODY, KT, B]) for g in range(2)]
        h_p = [sb(f"h_p{g}", [P, 2, KT, 2, B], F16) for g in range(2)]
        ps = ctx.enter_context(nc.psum_tensor("ps", [P, 8 * BANK], F32))

        wh_loaded = sem("wh_loaded")
        wx_loaded = sem("wx_loaded")
        x_loaded = sem("x_loaded")
        small_loaded = sem("small_loaded")
        consts_set = sem("consts_set")
        largest_found = sem("largest_found")
        largest_shared = sem("largest_shared")
        prep_chain = sem("prep_chain")
        pool_chain = sem("pool_chain")
        scales_set = sem("scales_set")
        weights_split = sem("weights_split")
        weights0_scaled = sem("weights0_scaled")
        weights0_high = sem("weights0_high")
        weights0_split = sem("weights0_split")
        bias_cleared = sem("bias_cleared")
        bias_split = sem("bias_split")
        out_stored = sem("out_stored")
        x_ready = [sem(f"x_ready{l}") for l in range(NL + 1)]
        out_ready = sem("out_ready")
        x_tmp_ready = [sem(f"x_tmp_ready{l}") for l in range(NL)]
        x_split = [sem(f"x_split{l}") for l in range(NL)]
        projected = [sem(f"projected{l}") for l in range(NL)]
        crit_done = [sem(f"crit_done{g}") for g in range(2)]
        rest_done = [sem(f"rest_done{g}") for g in range(2)]
        zc_ready = [sem(f"zc_ready{g}") for g in range(2)]
        zr_ready = [sem(f"zr_ready{g}") for g in range(2)]
        gates_ready = [sem(f"gates_ready{g}") for g in range(2)]
        rest_ready = [sem(f"rest_ready{g}") for g in range(2)]
        prod_ready = [sem(f"prod_ready{g}") for g in range(2)]
        cell_ready = [sem(f"cell_ready{g}") for g in range(2)]
        o_ready = [sem(f"o_ready{g}") for g in range(2)]
        tanh_c_ready = [sem(f"tanh_c_ready{g}") for g in range(2)]
        hist_ready = [sem(f"hist_ready{g}") for g in range(2)]
        h_ready = [sem(f"h_ready{g}") for g in range(2)]

        block = ctx.enter_context(nc.Block())

        def works(layer, s):
            return LAG[layer] <= s < LAG[layer] + T

        def stream_works(g, s):
            return any(works(l, s) for l in STREAMS[g])

        def rest_start(g):
            return LAG[STREAMS[g][0]]

        def crit_start(g):
            return LAG[STREAMS[g][1]]

        def all_steps(eng, body, first=0, last=STEPS):
            for s in range(first, LOOP_FROM):
                body(0, s, False)
            with eng.Fori(LOOP_FROM, LOOP_TO - BODY + 1, BODY) as base:
                for j in range(BODY):
                    body(base, j, True)
            for s in range(LOOP_TO, last):
                body(0, s, False)

        def time_of(base, j, steady):
            return LOOP_FROM + j if steady else j

        def lstm_window(s):
            return (s - LSTM_PHASE) // CH

        def crit_columns(g, s):
            w = lstm_window(s)
            return CRIT_BANK[g][w % 2] * BANK + (s - LSTM_PHASE) % CH * CRIT_STEP

        def o_columns(g, s):
            w = lstm_window(s)
            return O_BANK[w % 2] * BANK + g * REST_REGION + (s - LSTM_PHASE) % CH * REST_STEP

        def r_columns(g, s):
            return R_BANK[s // CH % 2] * BANK + g * REST_REGION + s % CH * REST_STEP

        def zc_view(g, s):
            c = CRIT_BANK[g][lstm_window(s) % 2] * BANK + CH * CRIT_STEP
            return ps[:, c:c + len(CRIT) * B]

        @block.sync
        def _(sp):
            for l in (0, 1):
                sp.dma_start(wh_f[:, :, TILE0[l] * P:(TILE0[l] + GATES[l]) * P],
                             wh[l].rearrange("(k p) n -> p k n", p=P)).then_inc(wh_loaded, 16)
                sp.dma_start(wx_f[:, :, TILE0[l] * P:(TILE0[l] + GATES[l]) * P],
                             wx[l].rearrange("(k p) n -> p k n", p=P)).then_inc(wx_loaded, 16)
            sp.dma_start(cond_f[:, :, :], cond).then_inc(small_loaded, 16)
            sp.dma_start(patt[:, :, :], pattern.rearrange("p (m c) -> p m c", m=NT)).then_inc(small_loaded, 16)
            sp.dma_start(half_c[:, :], half).then_inc(small_loaded, 16)
            sp.dma_start(x_all[:, :], x).then_inc(x_loaded, 16)

            def body(base, j, steady):
                s = time_of(base, j, steady)
                if s % CH == LSTM_PHASE + 1 and s >= LAG[3] + CH:
                    t = j - 1 - LAG[3]
                    p = (s - 1 - LAG[3]) // CH % 2
                    sp.wait_ge(out_ready, base + t)
                    sp.dma_start(out[:, bass.ds((base + (t - CH)) * (KT * B), CH * KT * B)],
                                 x_out[:, 1 - p, :]).then_inc(out_stored, 16)

            all_steps(sp, body, last=STEPS + 2)
            sp.wait_ge(out_stored, 16 * NCH)

        @block.gpsimd
        def _(pool):
            nc.gpsimd.memset(up[:, :], HSCALE).then_inc(consts_set, 1)
            nc.gpsimd.memset(down[:, :], 1.0 / HSCALE).then_inc(consts_set, 1)
            pool.wait_ge(largest_found, 3)
            nc.gpsimd.partition_all_reduce(largest_all[:, :], largest[:, :], P, bass.bass_isa.ReduceOp.max)\
                .then_inc(largest_shared, 1)
            pool.wait_ge(consts_set, 2)

            def flat(a, l, p):
                return a[l][:, p, :, :].rearrange("p k c -> p (k c)")

            def split_x(l, base, done, s_done):
                p = (s_done // CH - 1) % 2
                if s_done > CH:
                    pool.wait_ge(x_split[l], base + (done - CH))
                if s_done > BODY:
                    pool.wait_ge(projected[l], base + (done - BODY))
                pool.wait_ge(x_ready[l], base + done)
                nc.gpsimd.tensor_tensor(x_p[l][:, p, :, 0, :], xs[l][:, p, :, :], xsplit[:, :, :], ALU.mult)
                nc.gpsimd.tensor_tensor(xtmp[l][:, :, :], xs[l][:, p, :, :], xsplit[:, :, :], ALU.mult)\
                    .then_inc(x_tmp_ready[l], CH)
                pool.wait_ge(x_tmp_ready[l], base + done)
                nc.gpsimd.tensor_tensor(x_p[l][:, p, :, 1, :], xtmp[l][:, :, :], x_p[l][:, p, :, 0, :],
                                        ALU.subtract).then_inc(x_split[l], CH)

            def take_x(base, j, s):
                p = s // CH % 2
                if s >= BODY:
                    pool.wait_ge(x_ready[1], base + (j - CH))
                    pool.wait_ge(x_split[0], base + (j - CH))
                nc.gpsimd.tensor_tensor(flat(xs, 0, p), x_all[:, bass.ds((base + j) * (KT * B), CH * KT * B)],
                                        up[:, :], ALU.mult).then_inc(x_ready[0], CH)
                split_x(0, base, j + CH, s + CH)

            def residual(l, base, j, s):
                g = l // 2
                p = (s - LAG[l] - CH) // CH % 2
                done = j - LAG[l]
                pool.wait_ge(hist_ready[g], base + (j - rest_start(g)))
                if l < NL - 1:
                    if s - LAG[l] > BODY:
                        pool.wait_ge(x_ready[l + 2], base + (done - BODY))
                        pool.wait_ge(x_split[l + 1], base + (done - BODY))
                elif s - LAG[l] > CH:
                    pool.wait_ge(out_ready, base + (done - CH))
                slot = (s - CH) % BODY
                first = min(CH, BODY - slot)
                dst = xs[l + 1][:, p, :, :].rearrange("p k (t b) -> p t k b", b=B)
                src = xs[l][:, p, :, :].rearrange("p k (t b) -> p t k b", b=B)
                for a, z in ((0, first), (first, CH)):
                    if a < z:
                        at = (slot + a) % BODY
                        nc.gpsimd.tensor_tensor(dst[:, a:z], src[:, a:z],
                                                hist[g][:, l % 2, at:at + z - a, :, :], ALU.add)\
                            .then_inc(x_ready[l + 1], z - a)
                if l < NL - 1:
                    split_x(l + 1, base, done, s - LAG[l])
                if l == NL - 1:
                    pool.wait_ge(x_ready[NL], base + done)
                    if s - LAG[l] > CH:
                        pool.wait_ge(out_stored, base + (done - CH))
                    nc.gpsimd.tensor_tensor(x_out[:, p, :], flat(xs, NL, p), down[:, :], ALU.mult)\
                        .then_inc(out_ready, CH)

            pool.wait_ge(scales_set, 1)
            nc.gpsimd.tensor_scalar(xsplit[:, :, :].rearrange("p k c -> p (k c)"), up[:, :],
                                    inv[:, 1:2], TOP / HSCALE ** 2, ALU.mult, ALU.mult).then_inc(pool_chain, 1)
            pool.wait_ge(pool_chain, 1)
            pool.wait_ge(x_loaded, 16)
            take_x(0, 0, 0)

            chain = [1]
            for l in (1, 2, 3):
                for w, parts, w_scale in ((wx_f, wx_p, wx_scale), (wh_f, wh_p, wh_scale)):
                    c, z = TILE0[l] * P, (TILE0[l] + GATES[l]) * P
                    mid = c + SIGMOID_COLS if IS_LSTM[l] else c
                    for a, b, f in ((c, mid, 0.5), (mid, z, 1.0)):
                        if a < b:
                            for to in (parts[:, 0, :, a:b], w[:, :, a:b]):
                                last = nc.gpsimd.tensor_scalar(to, w[:, :, a:b], w_scale[:, :], f,
                                                               ALU.mult, ALU.mult)
                    last.then_inc(pool_chain, 1)
                    chain[0] += 1
                    pool.wait_ge(pool_chain, chain[0])
                    nc.gpsimd.tensor_tensor(parts[:, 1, :, c:z], w[:, :, c:z], parts[:, 0, :, c:z],
                                            ALU.subtract).then_inc(weights_split, 1)
                if l == 1:
                    take_x(0, CH, CH)

            def body(base, j, steady):
                s = time_of(base, j, steady)
                if s % CH == RNN_PHASE:
                    for l in (0, 2):
                        if steady or LAG[l] + CH <= s <= LAG[l] + T:
                            residual(l, base, j, s)
                if s % CH == 4 and s >= CH and (steady or s - 4 + CH < T):
                    take_x(base, j - 4 + CH, s - 4 + CH)
                if s % CH == LSTM_PHASE:
                    for l in (1, 3):
                        if steady or LAG[l] + CH <= s <= LAG[l] + T:
                            residual(l, base, j, s)

            all_steps(pool, body, last=STEPS + 1)

        @block.scalar
        def _(act):
            for l in (2, 3):
                act.dma_start(wh_f[:, :, TILE0[l] * P:(TILE0[l] + GATES[l]) * P],
                              wh[l].rearrange("(k p) n -> p k n", p=P)).then_inc(wh_loaded, 16)
            act.wait_ge(bias_cleared, 1)
            for q in range(3):
                for l in range(NL):
                    act.dma_start(bias_f[32 * q + TILE0[l]:32 * q + TILE0[l] + GATES[l], :],
                                  bias[l].rearrange("(m n) -> m n", n=P)).then_inc(small_loaded, 16)
            for l in (2, 3):
                act.dma_start(wx_f[:, :, TILE0[l] * P:(TILE0[l] + GATES[l]) * P],
                              wx[l].rearrange("(k p) n -> p k n", p=P)).then_inc(wx_loaded, 16)
            act.preload_act_table(TANH)
            act.wait_ge(weights0_scaled, 2)
            cols = slice(TILE0[0] * P, (TILE0[0] + GATES[0]) * P)
            for w, parts in ((wx_f, wx_p), (wh_f, wh_p)):
                nc.scalar.activation(parts[:, 0, :, cols], w[:, :, cols], COPY).then_inc(weights0_high, 1)
            act.wait_ge(scales_set, 1)
            z_factor = act.alloc_register("z_factor")
            act.reg_load(z_factor, z_scale[0:1, 0:1].bitcast(I32))

            def body(base, j, steady):
                s = time_of(base, j, steady)
                for g in range(2):
                    rnn, lstm = (works(l, s) for l in STREAMS[g])
                    if lstm:
                        act.wait_ge(zc_ready[g], base + (j - crit_start(g) + 1))
                        nc.scalar.activation(gates[g][:, 0:12], zc_view(g, s), TANH, scale=z_factor)\
                            .then_inc(gates_ready[g], 1)
                    if rnn or lstm:
                        act.wait_ge(zr_ready[g], base + (j - rest_start(g) + 1))
                        a, z = (0 if lstm else 4), (8 if rnn else 4)
                        nc.scalar.activation(rest[g][:, a:z], zr[g][:, a:z], TANH, scale=z_factor)\
                            .then_inc(rest_ready[g], 1)
                    if lstm:
                        act.wait_ge(cell_ready[g], base + (j - crit_start(g) + 1))
                        nc.scalar.activation(rest[g][:, 8:12], gates[g][:, 12:16], TANH, scale=0.5)\
                            .then_inc(tanh_c_ready[g], 1)

            all_steps(act, body)

        @block.vector
        def _(dve):
            for g in range(2):
                nc.vector.memset(gates[g][:, 12:16], 0.0)
                nc.vector.memset(mult[g][:, 0:4], HSCALE)
            nc.vector.memset(bias_f[:, :], 0.0).then_inc(bias_cleared, 1)
            chain = [0]

            def link(ins):
                chain[0] += 1
                ins.then_inc(prep_chain, 1)
                dve.wait_ge(prep_chain, chain[0])

            for n, (a, loaded, axes, count) in enumerate(((wh_f[:, :, :], wh_loaded, AX.XY, NL),
                                                          (wx_f[:, :, :], wx_loaded, AX.XY, NL),
                                                          (x_all[:, :], x_loaded, AX.X, 1))):
                dve.wait_ge(loaded, 16 * count)
                nc.vector.tensor_reduce(largest[:, n:n + 1], a, axes, ALU.max, apply_absolute_value=True)\
                    .then_inc(largest_found, 1)
            dve.wait_ge(largest_shared, 1)
            link(nc.vector.tensor_scalar(largest_all[:, 2:3], largest_all[:, 2:3], float(NL - 1), None, ALU.add))
            link(nc.vector.tensor_scalar(power[:, :].bitcast(I32), largest_all[:, :].bitcast(I32),
                                         EXPONENT_BITS, None, ALU.bitwise_and))
            link(nc.vector.tensor_tensor(x_w[:, :], power[:, 1:2], power[:, 2:3], ALU.mult))
            link(nc.vector.scalar_tensor_tensor(total[:, :], power[:, 0:1], LEAST_MAX, x_w[:, :], ALU.max, ALU.max))
            nc.vector.reciprocal(inv[:, 0:1], total[:, :])
            link(nc.vector.reciprocal(inv[:, 1:2], power[:, 2:3]))
            nc.vector.tensor_scalar(wh_scale[:, :], inv[:, 0:1], TOP, None, ALU.mult)
            nc.vector.tensor_scalar(wx_scale[:, :], inv[:, 0:1], power[:, 2:3], HSCALE, ALU.mult, ALU.mult)
            nc.vector.tensor_scalar(b_scale[:, :], inv[:, 0:1], TOP * HSCALE, None, ALU.mult)
            last = nc.vector.tensor_scalar(z_scale[:, :], total[:, :], 1.0 / (TOP * HSCALE), None, ALU.mult)
            last.then_inc(scales_set, 1)
            dve.wait_ge(scales_set, 1)
            cols = slice(TILE0[0] * P, (TILE0[0] + GATES[0]) * P)
            for w, w_scale in ((wx_f, wx_scale), (wh_f, wh_scale)):
                nc.vector.tensor_scalar(w[:, :, cols], w[:, :, cols], w_scale[:, :], None, ALU.mult)\
                    .then_inc(weights0_scaled, 1)
            dve.wait_ge(small_loaded, 16 * (3 + 3 * NL))
            link(nc.vector.tensor_scalar(cond_f[:, :, :], cond_f[:, :, :], HSCALE, None, ALU.mult))
            r = [bias_r[:, 0, :], bias_r[:, 1, :]]
            link(nc.vector.tensor_scalar(r[0], bias_f[:, :], b_scale[0:96, :], half_c[:, :],
                                         ALU.mult, ALU.mult))
            for q in range(3):
                link(nc.vector.tensor_copy(bias_s[:, q, :], r[q % 2]))
                if q < 2:
                    link(nc.vector.tensor_tensor(r[1 - q % 2], r[q % 2], bias_s[:, q, :], ALU.subtract))
            for q in range(3):
                rows = slice(32 * q, 32 * q + 32)
                last = nc.vector.tensor_copy(bias_p[rows, :], bias_s[rows, q, :])
            last.then_inc(bias_split, 1)
            for n, (w, parts) in enumerate(((wx_f, wx_p), (wh_f, wh_p))):
                dve.wait_ge(weights0_high, n + 1)
                nc.vector.tensor_tensor(parts[:, 1, :, cols], w[:, :, cols], parts[:, 0, :, cols],
                                        ALU.subtract).then_inc(weights0_split, 1)

            def reduce_crit(g, base, j, s):
                dve.wait_ge(crit_done[g], base + (j - crit_start(g) + 1))
                c = crit_columns(g, s)
                z = ps[:, c:c + CRIT_STEP].rearrange("p (m q b) -> p m b q", q=2, b=B)
                nc.vector.tensor_reduce(zc_view(g, s).rearrange("p (m b) -> p m b", b=B), z, AX.X, ALU.add)\
                    .then_inc(zc_ready[g], 1)

            def reduce_rest(g, base, j, s, rnn, lstm):
                dve.wait_ge(rest_done[g], base + (j - rest_start(g) + 1))
                o, r = o_columns(g, s), r_columns(g, s)
                dst = zr[g][:, :].rearrange("p (l m b) -> p l m b", l=2, b=B)
                z = ps[:, o:o + REST_STEP]
                spans = [(o, 0, 2, r - o)] if rnn and lstm and abs(o - r) < 2 * BANK else \
                    [(o, 0, 1, 1)] * lstm + [(r, 1, 1, 1)] * rnn
                for c, l, n, stride in spans:
                    z = ps[:, c:c + REST_STEP]
                    z = bass.AP(z.tensor, z.offset, [list(z.ap[0]), [stride, n], [COLS, KT], [1, B], [B, 2]])
                    last = nc.vector.tensor_reduce(dst[:, l:l + n], z, AX.X, ALU.add)
                last.then_inc(zr_ready[g], 1)

            def products(g, base, j):
                dve.wait_ge(gates_ready[g], base + (j - crit_start(g) + 1))
                nc.vector.scalar_tensor_tensor(prod[g][:, :], gates[g][:, 0:8], 1.0, gates[g][:, 8:16],
                                               ALU.add, ALU.mult).then_inc(prod_ready[g], 1)

            def cell(g, base, j):
                dve.wait_ge(prod_ready[g], base + (j - crit_start(g) + 1))
                nc.vector.scalar_tensor_tensor(gates[g][:, 12:16], prod[g][:, 4:8], 0.5, prod[g][:, 0:4],
                                               ALU.mult, ALU.add).then_inc(cell_ready[g], 1)

            def o_gate(g, base, j):
                dve.wait_ge(rest_ready[g], base + (j - rest_start(g) + 1))
                nc.vector.tensor_scalar(mult[g][:, 4:8], rest[g][:, 0:4], 1.0, 0.5 * HSCALE,
                                        ALU.add, ALU.mult).then_inc(o_ready[g], 1)

            def h_views(g, s, rnn, lstm):
                lay = slice(0 if rnn else 1, 2 if lstm else 1)
                n = KT * B
                a, z = lay.start * n, lay.stop * n
                ins = (mult[g][:, a:z].rearrange("p (l k b) -> p l k b", k=KT, b=B),
                       rest[g][:, 4 + a:4 + z].rearrange("p (l k b) -> p l k b", k=KT, b=B))
                return ins, hist[g][:, lay, s % BODY, :, :], h_p[g][:, lay, :, 0, :], h_p[g][:, lay, :, 1, :]

            def hidden(g, base, j, s, rnn, lstm):
                if lstm:
                    dve.wait_ge(o_ready[g], base + (j - crit_start(g) + 1))
                    dve.wait_ge(tanh_c_ready[g], base + (j - crit_start(g) + 1))
                else:
                    dve.wait_ge(rest_ready[g], base + (j - rest_start(g) + 1))
                for l in STREAMS[g]:
                    if works(l, s) and (s - LAG[l]) % CH == 0 and s - LAG[l] >= BODY:
                        dve.wait_ge(x_ready[l + 1], base + (j - LAG[l] - CH))
                (m, t), hf, high, _ = h_views(g, s, rnn, lstm)
                nc.vector.tensor_tensor(high, m, t, ALU.mult)
                nc.vector.tensor_tensor(hf, m, t, ALU.mult).then_inc(hist_ready[g], 1)

            def hidden_low(g, base, j, s, rnn, lstm):
                dve.wait_ge(hist_ready[g], base + (j - rest_start(g) + 1))
                _, hf, high, low = h_views(g, s, rnn, lstm)
                nc.vector.tensor_tensor(low, hf, high, ALU.subtract).then_inc(h_ready[g], 1)

            def body(base, j, steady):
                s = time_of(base, j, steady)
                now = [[works(l, s) for l in STREAMS[g]] for g in range(2)]
                before = [works(l, s - 1) for l in STREAMS[1]]
                (rnn_a, lstm_a), (rnn_b, lstm_b) = now
                if any(before):
                    hidden(1, base, j - 1, s - 1, *before)
                if lstm_a:
                    reduce_crit(0, base, j, s)
                if any(before):
                    hidden_low(1, base, j - 1, s - 1, *before)
                if lstm_a:
                    products(0, base, j)
                if rnn_a or lstm_a:
                    reduce_rest(0, base, j, s, rnn_a, lstm_a)
                if lstm_a:
                    cell(0, base, j)
                    o_gate(0, base, j)
                if rnn_a or lstm_a:
                    hidden(0, base, j, s, rnn_a, lstm_a)
                if lstm_b:
                    reduce_crit(1, base, j, s)
                if rnn_a or lstm_a:
                    hidden_low(0, base, j, s, rnn_a, lstm_a)
                if lstm_b:
                    products(1, base, j)
                if rnn_b or lstm_b:
                    reduce_rest(1, base, j, s, rnn_b, lstm_b)
                if lstm_b:
                    cell(1, base, j)
                    o_gate(1, base, j)

            all_steps(dve, body, last=STEPS + 1)

        @block.tensor
        def _(pe):
            def weights(w, l, tile, kt):
                c = (TILE0[l] + tile) * P
                return w[:, kt, c:c + P]

            def recurrent(l, tiles, c, first, base, j, done):
                g, lay = l // 2, l % 2
                for m, tile in enumerate(tiles):
                    for kt in range(KT):
                        if first:
                            last = nc.tensor.matmul(ps[:, c + m * COLS:c + m * COLS + B],
                                                    weights(wh_f, l, tile, kt), cond_f[:, kt, :],
                                                    start=False, stop=True, skip_group_check=True)
                            continue
                        for part in range(2):
                            last = nc.tensor.matmul(ps[:, c + m * COLS:c + (m + 1) * COLS],
                                                    weights(wh_p[:, part], l, tile, kt),
                                                    h_p[g][:, lay, kt, :, :],
                                                    start=False, stop=True, skip_group_check=True)
                if done is not None:
                    last.then_inc(done, 1)

            def chunk_columns(l, tile, s):
                if not IS_LSTM[l]:
                    c, m, step = r_columns(l // 2, s), tile, REST_STEP
                elif tile in CRIT:
                    c, m, step = crit_columns(l // 2, s), CRIT.index(tile), CRIT_STEP
                else:
                    c, m, step = o_columns(l // 2, s), OGATE.index(tile), REST_STEP
                z = ps[:, c:c + CH * step].rearrange("p (t m q b) -> p m q t b", t=CH, q=2, b=B)
                return z[:, m]

            def bias_fill(layers, tiles, s):
                start = True
                for l in layers:
                    if works(l, s):
                        for tile in tiles:
                            nc.tensor.matmul(chunk_columns(l, tile, s)[:, 0], bias_p[:, :],
                                             patt[:, TILE0[l] + tile, :],
                                             start=start, stop=True, skip_group_check=True)
                            start = False

            def project(l, tile, kt, base, j, s, begins, ends):
                if begins:
                    pe.wait_ge(x_split[l], base + (j - LAG[l] + CH))
                p = (s - LAG[l]) // CH % 2
                for part in range(2):
                    mm = nc.tensor.matmul(chunk_columns(l, tile, s), weights(wx_p[:, part], l, tile, kt),
                                          x_p[l][:, p, kt, :, :].rearrange("p q c -> p (q c)"),
                                          start=False, stop=True, skip_group_check=True)
                if ends:
                    mm.then_inc(projected[l], CH)

            order = {True: CRIT + OGATE, False: RNN_TILES}

            def fill_jobs(phase):
                lstm = [(l, t, k) for l in (1, 3) for t in order[True] for k in range(KT)]
                rnn = [(l, t, k) for l in (0, 2) for t in order[False] for k in range(KT)]
                if 1 <= phase <= 11:
                    return lstm[3 * (phase - 1):3 * phase]
                if phase == 12:
                    return rnn[0:3]
                if phase == 13:
                    return rnn[3:5]
                if phase == 14:
                    return rnn[5:8]
                return []

            bias_jobs = {0: ((0, 2), RNN_TILES, CH), 
                         13: ((1,), CRIT, LSTM_PHASE + CH - 13), 14: ((3,), CRIT, LSTM_PHASE + CH - 14),
                         15: ((1, 3), OGATE, LSTM_PHASE + CH - 15)}

            def fill(base, j, s, steady, half):
                phase = s % CH
                if half == 0 and phase in bias_jobs:
                    layers, tiles, at = bias_jobs[phase]
                    bias_fill(layers, tiles, s + at)
                jobs = fill_jobs(phase)
                for l, tile, kt in (jobs[1:] if half else jobs[:1]):
                    at = (LSTM_PHASE if IS_LSTM[l] else CH) - phase
                    start = s + at
                    if not works(l, start):
                        continue
                    tiles = order[IS_LSTM[l]]
                    if start == LAG[l] and l and (tile, kt) == (tiles[0], 0):
                        pe.wait_ge(weights_split, 2 * l)
                    project(l, tile, kt, base, j + at, start, (tile, kt) == (tiles[0], 0),
                            (tile, kt) == (tiles[-1], KT - 1))

            pe.wait_ge(bias_split, 1)
            bias_fill((0,), RNN_TILES, 0)
            pe.wait_ge(weights0_split, 2)
            for tile in RNN_TILES:
                for kt in range(KT):
                    project(0, tile, kt, 0, 0, 0, (tile, kt) == (0, 0), (tile, kt) == (RNN_TILES[-1], KT - 1))

            def body(base, j, steady):
                s = time_of(base, j, steady)
                for g in range(2):
                    rnn_l, lstm_l = STREAMS[g]
                    rnn, lstm = works(rnn_l, s), works(lstm_l, s)
                    if (rnn or lstm) and (steady or s > rest_start(g)):
                        pe.wait_ge(h_ready[g], base + (j - rest_start(g)))
                    if lstm:
                        recurrent(lstm_l, CRIT, crit_columns(g, s), s == LAG[lstm_l], base, j, crit_done[g])
                    if rnn or lstm:
                        if g == 1:
                            if stream_works(0, s):
                                pe.wait_ge(zr_ready[0], base + (j + 1))
                        elif stream_works(1, s - 1):
                            pe.wait_ge(zr_ready[1], base + (j - rest_start(1)))
                    if lstm:
                        recurrent(lstm_l, OGATE, o_columns(g, s), s == LAG[lstm_l], base, j,
                                  None if rnn else rest_done[g])
                    if rnn:
                        recurrent(rnn_l, RNN_TILES, r_columns(g, s), s == LAG[rnn_l], base, j, rest_done[g])
                    fill(base, j, s, steady, g)

            all_steps(pe, body)


def kernel(x, cond_1024, L0_cond_Wx, L0_cond_Wh, L0_cond_b, L1_cond_Wx, L1_cond_Wh, L1_cond_b,
           L2_cond_Wx, L2_cond_Wh, L2_cond_b, L3_cond_Wx, L3_cond_Wh, L3_cond_b):
    import ml_dtypes
    import concourse.bacc as bacc
    from concourse.bass_utils import run_bass_kernel_spmd

    nc = bacc.Bacc("TRN2", target_bir_lowering=False, num_devices=1)
    xt = np.asarray(x).reshape(B, NCH, CH, KT, P).transpose(4, 1, 3, 2, 0).reshape(P, -1)
    arrays = {
        "x": xt,
        "cond": np.asarray(cond_1024).reshape(B, KT, P).transpose(2, 1, 0),
        "Wx0": L0_cond_Wx, "Wx1": L1_cond_Wx, "Wx2": L2_cond_Wx, "Wx3": L3_cond_Wx,
        "Wh0": L0_cond_Wh, "Wh1": L1_cond_Wh, "Wh2": L2_cond_Wh, "Wh3": L3_cond_Wh,
        "b0": L0_cond_b, "b1": L1_cond_b, "b2": L2_cond_b, "b3": L3_cond_b,
        "pattern": bias_patterns().astype(ml_dtypes.bfloat16),
    }
    half = np.ones((3, 32, 1), np.float32)
    for l in range(NL):
        if IS_LSTM[l]:
            half[:, TILE0[l]:TILE0[l] + SIGMOID_COLS // P] = 0.5
    arrays["half"] = half.reshape(96, 1)
    arrays = {k: np.ascontiguousarray(v) for k, v in arrays.items()}
    ap = {k: nc.dram_tensor(k, v.shape, mybir.dt.from_np(v.dtype), kind="ExternalInput").ap()
          for k, v in arrays.items()}
    out = nc.dram_tensor("out", (P, T * KT * B), F32, kind="ExternalOutput").ap()
    build(nc, ap["x"], ap["cond"], [ap[f"Wx{l}"] for l in range(NL)], [ap[f"Wh{l}"] for l in range(NL)],
          [ap[f"b{l}"] for l in range(NL)], ap["pattern"], ap["half"], out)
    r = run_bass_kernel_spmd(nc, [arrays], core_ids=[0])
    y = np.asarray(r.results[0]["out"]).reshape(P, NCH, KT, CH, B)
    return np.ascontiguousarray(y.transpose(4, 1, 3, 2, 0).reshape(B, T, D))
```

```python
from contextlib import ExitStack

import numpy as np

import concourse.bass as bass
from concourse import mybir

F32 = mybir.dt.float32
F16 = mybir.dt.float16
BF16 = mybir.dt.bfloat16
I32 = mybir.dt.int32
ALU = mybir.AluOpType
TANH = mybir.ActivationFunctionType.Tanh
COPY = mybir.ActivationFunctionType.Copy
AX = mybir.AxisListType

P = 128
B, T, D = 2, 1024, 256
KT = D // P
CH = 16
NCH = T // CH
BODY = 2 * CH
NL = 4
IS_LSTM = [False, True, False, True]
LAG = [0, 28, 48, 76]
RNN_PHASE = LAG[0] % CH
LSTM_PHASE = LAG[1] % CH
STREAMS = [(0, 1), (2, 3)]
STEPS = LAG[3] + T
LOOP_FROM = 3 * BODY
LOOP_TO = T - BODY

HSCALE = 2.0 ** 14
TOP = 2.0 ** 14
LEAST_MAX = 2.0 ** -20
EXPONENT_BITS = 0x7F800000

GATES = [4 * KT if lstm else KT for lstm in IS_LSTM]
TILE0 = [0, GATES[0], GATES[0] + GATES[1], GATES[0] + GATES[1] + GATES[2]]
NT = sum(GATES)
CRIT = [0, 1, 2, 3, 6, 7]
OGATE = [4, 5]
RNN_TILES = [0, 1]
SIGMOID_COLS = 3 * D

BANK = 512
COLS = 2 * B
CRIT_STEP = len(CRIT) * COLS
REST_STEP = KT * COLS
CRIT_BANK = [[0, 1], [2, 3]]
O_BANK = [4, 5]
R_BANK = [6, 7]
REST_REGION = CH * REST_STEP


def bias_patterns():
    out = np.zeros((3, 32, NT, CH * B), np.float32)
    for tile in range(NT):
        out[:, tile, tile] = 1.0
    return out.reshape(96, -1)


def build(nc, x, cond, wx, wh, bias, pattern, half, out):
    ctx = ExitStack()
    with ctx:
        def sb(name, shape, dt=F32):
            return ctx.enter_context(nc.sbuf_tensor(name, shape, dt))

        def sem(name):
            return ctx.enter_context(nc.semaphore(name))

        wh_f = sb("wh_f", [P, KT, NT * P])
        wx_f = sb("wx_f", [P, KT, NT * P])
        wh_p = sb("wh_p", [P, 2, KT, NT * P], F16)
        cond_f = sb("cond_f", [P, KT, B])
        bias_f = sb("bias_f", [96, P])
        bias_r = sb("bias_r", [96, 2, P])
        bias_s = sb("bias_s", [96, 3, P], BF16)
        bias_p = sb("bias_p", [96, P], BF16)
        patt = sb("patt", [96, NT, CH * B], BF16)
        half_c = sb("half_c", [96, 1])
        largest = sb("largest", [P, 3])
        largest_all = sb("largest_all", [P, 3])
        power = sb("power", [P, 3])
        x_w = sb("x_w", [P, 1])
        total = sb("total", [P, 1])
        inv = sb("inv", [P, 2])
        wh_scale = sb("wh_scale", [P, 1])
        wx_scale = sb("wx_scale", [P, 1])
        b_scale = sb("b_scale", [P, 1])
        z_scale = sb("z_scale", [P, 1])
        up = sb("up", [P, KT * CH * B])
        down = sb("down", [P, KT * CH * B])
        xsplit = sb("xsplit", [P, KT, CH * B])
        x_all = sb("x_all", [P, T * KT * B])
        wx_p = sb("wx_p", [P, 2, KT, NT * P], F16)
        xtmp = [sb(f"xtmp{l}", [P, KT, CH * B]) for l in range(NL)]
        x_p = [sb(f"x_p{l}", [P, 2, KT, 2, CH * B], F16) for l in range(NL)]
        xs = [sb(f"x{l}", [P, 2, KT, CH * B]) for l in range(NL + 1)]
        x_out = sb("x_out", [P, 2, KT * CH * B])
        zo = [sb(f"zo{g}", [P, KT * B]) for g in range(2)]
        zr = [sb(f"zr{g}", [P, KT * B]) for g in range(2)]
        gates = [sb(f"gates{g}", [P, 16]) for g in range(2)]
        rest = [sb(f"rest{g}", [P, 12]) for g in range(2)]
        mult = [sb(f"mult{g}", [P, 8]) for g in range(2)]
        prod = [sb(f"prod{g}", [P, 8]) for g in range(2)]
        hist = [sb(f"hist{g}", [P, 2, BODY, KT, B]) for g in range(2)]
        h_p = [sb(f"h_p{g}", [P, 2, KT, 2, B], F16) for g in range(2)]
        ps = ctx.enter_context(nc.psum_tensor("ps", [P, 8 * BANK], F32))

        wh_loaded = sem("wh_loaded")
        wx_loaded = sem("wx_loaded")
        x_loaded = sem("x_loaded")
        small_loaded = sem("small_loaded")
        consts_set = sem("consts_set")
        largest_found = sem("largest_found")
        largest_shared = sem("largest_shared")
        prep_chain = sem("prep_chain")
        pool_chain = sem("pool_chain")
        scales_set = sem("scales_set")
        weights_split = sem("weights_split")
        weights0_scaled = sem("weights0_scaled")
        weights0_high = sem("weights0_high")
        weights0_split = sem("weights0_split")
        bias_cleared = sem("bias_cleared")
        bias_split = sem("bias_split")
        out_stored = sem("out_stored")
        x_ready = [sem(f"x_ready{l}") for l in range(NL + 1)]
        out_ready = sem("out_ready")
        x_tmp_ready = [sem(f"x_tmp_ready{l}") for l in range(NL)]
        x_split = [sem(f"x_split{l}") for l in range(NL)]
        projected = [sem(f"projected{l}") for l in range(NL)]
        crit_done = [sem(f"crit_done{g}") for g in range(2)]
        o_done = [sem(f"o_done{g}") for g in range(2)]
        rnn_done = [sem(f"rnn_done{g}") for g in range(2)]
        zc_ready = [sem(f"zc_ready{g}") for g in range(2)]
        zo_ready = [sem(f"zo_ready{g}") for g in range(2)]
        zr_ready = [sem(f"zr_ready{g}") for g in range(2)]
        gates_ready = [sem(f"gates_ready{g}") for g in range(2)]
        tanh_o_ready = [sem(f"tanh_o_ready{g}") for g in range(2)]
        tanh_r_ready = [sem(f"tanh_r_ready{g}") for g in range(2)]
        prod_ready = [sem(f"prod_ready{g}") for g in range(2)]
        cell_ready = [sem(f"cell_ready{g}") for g in range(2)]
        tanh_c_ready = [sem(f"tanh_c_ready{g}") for g in range(2)]
        hist_ready = [sem(f"hist_ready{g}") for g in range(2)]
        h_ready = [sem(f"h_ready{g}") for g in range(2)]

        block = ctx.enter_context(nc.Block())

        def works(layer, s):
            return LAG[layer] <= s < LAG[layer] + T

        def stream_works(g, s):
            return any(works(l, s) for l in STREAMS[g])

        def rest_start(g):
            return LAG[STREAMS[g][0]]

        def crit_start(g):
            return LAG[STREAMS[g][1]]

        def all_steps(eng, body, first=0, last=STEPS):
            for s in range(first, LOOP_FROM):
                body(0, s, False)
            with eng.Fori(LOOP_FROM, LOOP_TO - BODY + 1, BODY) as base:
                for j in range(BODY):
                    body(base, j, True)
            for s in range(LOOP_TO, last):
                body(0, s, False)

        def time_of(base, j, steady):
            return LOOP_FROM + j if steady else j

        def lstm_window(s):
            return (s - LSTM_PHASE) // CH

        def crit_columns(g, s):
            w = lstm_window(s)
            return CRIT_BANK[g][w % 2] * BANK + (s - LSTM_PHASE) % CH * CRIT_STEP

        def o_columns(g, s):
            w = lstm_window(s)
            return O_BANK[w % 2] * BANK + g * REST_REGION + (s - LSTM_PHASE) % CH * REST_STEP

        def r_columns(g, s):
            return R_BANK[s // CH % 2] * BANK + g * REST_REGION + s % CH * REST_STEP

        def zc_view(g, s):
            c = CRIT_BANK[g][lstm_window(s) % 2] * BANK + CH * CRIT_STEP
            return ps[:, c:c + len(CRIT) * B]

        @block.sync
        def _(sp):
            for l in (0, 1):
                sp.dma_start(wh_f[:, :, TILE0[l] * P:(TILE0[l] + GATES[l]) * P],
                             wh[l].rearrange("(k p) n -> p k n", p=P)).then_inc(wh_loaded, 16)
                sp.dma_start(wx_f[:, :, TILE0[l] * P:(TILE0[l] + GATES[l]) * P],
                             wx[l].rearrange("(k p) n -> p k n", p=P)).then_inc(wx_loaded, 16)
            sp.dma_start(cond_f[:, :, :], cond).then_inc(small_loaded, 16)
            sp.dma_start(patt[:, :, :], pattern.rearrange("p (m c) -> p m c", m=NT)).then_inc(small_loaded, 16)
            sp.dma_start(half_c[:, :], half).then_inc(small_loaded, 16)
            sp.dma_start(x_all[:, :], x).then_inc(x_loaded, 16)

            def body(base, j, steady):
                s = time_of(base, j, steady)
                if s % CH == LSTM_PHASE + 1 and s >= LAG[3] + CH:
                    t = j - 1 - LAG[3]
                    p = (s - 1 - LAG[3]) // CH % 2
                    sp.wait_ge(out_ready, base + t)
                    sp.dma_start(out[:, bass.ds((base + (t - CH)) * (KT * B), CH * KT * B)],
                                 x_out[:, 1 - p, :]).then_inc(out_stored, 16)

            all_steps(sp, body, last=STEPS + 2)
            sp.wait_ge(out_stored, 16 * NCH)

        @block.gpsimd
        def _(pool):
            nc.gpsimd.memset(up[:, :], HSCALE).then_inc(consts_set, 1)
            nc.gpsimd.memset(down[:, :], 1.0 / HSCALE).then_inc(consts_set, 1)
            pool.wait_ge(largest_found, 3)
            nc.gpsimd.partition_all_reduce(largest_all[:, :], largest[:, :], P, bass.bass_isa.ReduceOp.max)\
                .then_inc(largest_shared, 1)
            pool.wait_ge(consts_set, 2)

            def flat(a, l, p):
                return a[l][:, p, :, :].rearrange("p k c -> p (k c)")

            def split_x(l, base, done, s_done):
                p = (s_done // CH - 1) % 2
                if s_done > CH:
                    pool.wait_ge(x_split[l], base + (done - CH))
                if s_done > BODY:
                    pool.wait_ge(projected[l], base + (done - BODY))
                pool.wait_ge(x_ready[l], base + done)
                nc.gpsimd.tensor_tensor(x_p[l][:, p, :, 0, :], xs[l][:, p, :, :], xsplit[:, :, :], ALU.mult)
                nc.gpsimd.tensor_tensor(xtmp[l][:, :, :], xs[l][:, p, :, :], xsplit[:, :, :], ALU.mult)\
                    .then_inc(x_tmp_ready[l], CH)
                pool.wait_ge(x_tmp_ready[l], base + done)
                nc.gpsimd.tensor_tensor(x_p[l][:, p, :, 1, :], xtmp[l][:, :, :], x_p[l][:, p, :, 0, :],
                                        ALU.subtract).then_inc(x_split[l], CH)

            def take_x(base, j, s):
                p = s // CH % 2
                if s >= BODY:
                    pool.wait_ge(x_ready[1], base + (j - CH))
                    pool.wait_ge(x_split[0], base + (j - CH))
                nc.gpsimd.tensor_tensor(flat(xs, 0, p), x_all[:, bass.ds((base + j) * (KT * B), CH * KT * B)],
                                        up[:, :], ALU.mult).then_inc(x_ready[0], CH)
                split_x(0, base, j + CH, s + CH)

            def residual(l, base, j, s):
                g = l // 2
                p = (s - LAG[l] - CH) // CH % 2
                done = j - LAG[l]
                pool.wait_ge(hist_ready[g], base + (j - rest_start(g)))
                if l < NL - 1:
                    if s - LAG[l] > BODY:
                        pool.wait_ge(x_ready[l + 2], base + (done - BODY))
                        pool.wait_ge(x_split[l + 1], base + (done - BODY))
                elif s - LAG[l] > CH:
                    pool.wait_ge(out_ready, base + (done - CH))
                slot = (s - CH) % BODY
                first = min(CH, BODY - slot)
                dst = xs[l + 1][:, p, :, :].rearrange("p k (t b) -> p t k b", b=B)
                src = xs[l][:, p, :, :].rearrange("p k (t b) -> p t k b", b=B)
                for a, z in ((0, first), (first, CH)):
                    if a < z:
                        at = (slot + a) % BODY
                        nc.gpsimd.tensor_tensor(dst[:, a:z], src[:, a:z],
                                                hist[g][:, l % 2, at:at + z - a, :, :], ALU.add)\
                            .then_inc(x_ready[l + 1], z - a)
                if l < NL - 1:
                    split_x(l + 1, base, done, s - LAG[l])
                if l == NL - 1:
                    pool.wait_ge(x_ready[NL], base + done)
                    if s - LAG[l] > CH:
                        pool.wait_ge(out_stored, base + (done - CH))
                    nc.gpsimd.tensor_tensor(x_out[:, p, :], flat(xs, NL, p), down[:, :], ALU.mult)\
                        .then_inc(out_ready, CH)

            pool.wait_ge(scales_set, 1)
            nc.gpsimd.tensor_scalar(xsplit[:, :, :].rearrange("p k c -> p (k c)"), up[:, :],
                                    inv[:, 1:2], TOP / HSCALE ** 2, ALU.mult, ALU.mult).then_inc(pool_chain, 1)
            pool.wait_ge(pool_chain, 1)
            pool.wait_ge(x_loaded, 16)
            take_x(0, 0, 0)

            chain = [1]
            for l in (1, 2, 3):
                for w, parts, w_scale in ((wx_f, wx_p, wx_scale), (wh_f, wh_p, wh_scale)):
                    c, z = TILE0[l] * P, (TILE0[l] + GATES[l]) * P
                    mid = c + SIGMOID_COLS if IS_LSTM[l] else c
                    for a, b, f in ((c, mid, 0.5), (mid, z, 1.0)):
                        if a < b:
                            for to in (parts[:, 0, :, a:b], w[:, :, a:b]):
                                last = nc.gpsimd.tensor_scalar(to, w[:, :, a:b], w_scale[:, :], f,
                                                               ALU.mult, ALU.mult)
                    last.then_inc(pool_chain, 1)
                    chain[0] += 1
                    pool.wait_ge(pool_chain, chain[0])
                    nc.gpsimd.tensor_tensor(parts[:, 1, :, c:z], w[:, :, c:z], parts[:, 0, :, c:z],
                                            ALU.subtract).then_inc(weights_split, 1)
                if l == 1:
                    take_x(0, CH, CH)

            def body(base, j, steady):
                s = time_of(base, j, steady)
                if s % CH == RNN_PHASE:
                    for l in (0, 2):
                        if steady or LAG[l] + CH <= s <= LAG[l] + T:
                            residual(l, base, j, s)
                if s % CH == 4 and s >= CH and (steady or s - 4 + CH < T):
                    take_x(base, j - 4 + CH, s - 4 + CH)
                if s % CH == LSTM_PHASE:
                    for l in (1, 3):
                        if steady or LAG[l] + CH <= s <= LAG[l] + T:
                            residual(l, base, j, s)

            all_steps(pool, body, last=STEPS + 1)

        @block.scalar
        def _(act):
            for l in (2, 3):
                act.dma_start(wh_f[:, :, TILE0[l] * P:(TILE0[l] + GATES[l]) * P],
                              wh[l].rearrange("(k p) n -> p k n", p=P)).then_inc(wh_loaded, 16)
            act.wait_ge(bias_cleared, 1)
            for q in range(3):
                for l in range(NL):
                    act.dma_start(bias_f[32 * q + TILE0[l]:32 * q + TILE0[l] + GATES[l], :],
                                  bias[l].rearrange("(m n) -> m n", n=P)).then_inc(small_loaded, 16)
            for l in (2, 3):
                act.dma_start(wx_f[:, :, TILE0[l] * P:(TILE0[l] + GATES[l]) * P],
                              wx[l].rearrange("(k p) n -> p k n", p=P)).then_inc(wx_loaded, 16)
            act.preload_act_table(TANH)
            act.wait_ge(weights0_scaled, 2)
            cols = slice(TILE0[0] * P, (TILE0[0] + GATES[0]) * P)
            for w, parts in ((wx_f, wx_p), (wh_f, wh_p)):
                nc.scalar.activation(parts[:, 0, :, cols], w[:, :, cols], COPY).then_inc(weights0_high, 1)
            act.wait_ge(scales_set, 1)
            z_factor = act.alloc_register("z_factor")
            act.reg_load(z_factor, z_scale[0:1, 0:1].bitcast(I32))

            def body(base, j, steady):
                s = time_of(base, j, steady)
                for g in range(2):
                    rnn, lstm = (works(l, s) for l in STREAMS[g])
                    if lstm:
                        act.wait_ge(zc_ready[g], base + (j - crit_start(g) + 1))
                        nc.scalar.activation(gates[g][:, 0:12], zc_view(g, s), TANH, scale=z_factor)\
                            .then_inc(gates_ready[g], 1)
                        act.wait_ge(zo_ready[g], base + (j - crit_start(g) + 1))
                        nc.scalar.activation(rest[g][:, 0:4], zo[g][:, :], TANH, scale=z_factor)\
                            .then_inc(tanh_o_ready[g], 1)
                    if rnn:
                        act.wait_ge(zr_ready[g], base + (j - rest_start(g) + 1))
                        nc.scalar.activation(rest[g][:, 4:8], zr[g][:, :], TANH, scale=z_factor)\
                            .then_inc(tanh_r_ready[g], 1)
                    if lstm:
                        act.wait_ge(tanh_o_ready[g], base + (j - crit_start(g) + 1))
                        nc.scalar.activation(mult[g][:, 4:8], rest[g][:, 0:4], COPY,
                                             bias=0.5 * HSCALE, scale=0.5 * HSCALE)
                    if lstm:
                        act.wait_ge(cell_ready[g], base + (j - crit_start(g) + 1))
                        nc.scalar.activation(rest[g][:, 8:12], gates[g][:, 12:16], TANH, scale=0.5)\
                            .then_inc(tanh_c_ready[g], 1)

            all_steps(act, body)

        @block.vector
        def _(dve):
            for g in range(2):
                nc.vector.memset(gates[g][:, 12:16], 0.0)
                nc.vector.memset(mult[g][:, 0:4], HSCALE)
            nc.vector.memset(bias_f[:, :], 0.0).then_inc(bias_cleared, 1)
            chain = [0]

            def link(ins):
                chain[0] += 1
                ins.then_inc(prep_chain, 1)
                dve.wait_ge(prep_chain, chain[0])

            for n, (a, loaded, axes, count) in enumerate(((wh_f[:, :, :], wh_loaded, AX.XY, NL),
                                                          (wx_f[:, :, :], wx_loaded, AX.XY, NL),
                                                          (x_all[:, :], x_loaded, AX.X, 1))):
                dve.wait_ge(loaded, 16 * count)
                nc.vector.tensor_reduce(largest[:, n:n + 1], a, axes, ALU.max, apply_absolute_value=True)\
                    .then_inc(largest_found, 1)
            dve.wait_ge(largest_shared, 1)
            link(nc.vector.tensor_scalar(largest_all[:, 2:3], largest_all[:, 2:3], float(NL - 1), None, ALU.add))
            link(nc.vector.tensor_scalar(power[:, :].bitcast(I32), largest_all[:, :].bitcast(I32),
                                         EXPONENT_BITS, None, ALU.bitwise_and))
            link(nc.vector.tensor_tensor(x_w[:, :], power[:, 1:2], power[:, 2:3], ALU.mult))
            link(nc.vector.scalar_tensor_tensor(total[:, :], power[:, 0:1], LEAST_MAX, x_w[:, :], ALU.max, ALU.max))
            nc.vector.reciprocal(inv[:, 0:1], total[:, :])
            link(nc.vector.reciprocal(inv[:, 1:2], power[:, 2:3]))
            nc.vector.tensor_scalar(wh_scale[:, :], inv[:, 0:1], TOP, None, ALU.mult)
            nc.vector.tensor_scalar(wx_scale[:, :], inv[:, 0:1], power[:, 2:3], HSCALE, ALU.mult, ALU.mult)
            nc.vector.tensor_scalar(b_scale[:, :], inv[:, 0:1], TOP * HSCALE, None, ALU.mult)
            last = nc.vector.tensor_scalar(z_scale[:, :], total[:, :], 1.0 / (TOP * HSCALE), None, ALU.mult)
            last.then_inc(scales_set, 1)
            dve.wait_ge(scales_set, 1)
            cols = slice(TILE0[0] * P, (TILE0[0] + GATES[0]) * P)
            for w, w_scale in ((wx_f, wx_scale), (wh_f, wh_scale)):
                nc.vector.tensor_scalar(w[:, :, cols], w[:, :, cols], w_scale[:, :], None, ALU.mult)\
                    .then_inc(weights0_scaled, 1)
            dve.wait_ge(small_loaded, 16 * (3 + 3 * NL))
            link(nc.vector.tensor_scalar(cond_f[:, :, :], cond_f[:, :, :], HSCALE, None, ALU.mult))
            r = [bias_r[:, 0, :], bias_r[:, 1, :]]
            link(nc.vector.tensor_scalar(r[0], bias_f[:, :], b_scale[0:96, :], half_c[:, :],
                                         ALU.mult, ALU.mult))
            for q in range(3):
                link(nc.vector.tensor_copy(bias_s[:, q, :], r[q % 2]))
                if q < 2:
                    link(nc.vector.tensor_tensor(r[1 - q % 2], r[q % 2], bias_s[:, q, :], ALU.subtract))
            for q in range(3):
                rows = slice(32 * q, 32 * q + 32)
                last = nc.vector.tensor_copy(bias_p[rows, :], bias_s[rows, q, :])
            last.then_inc(bias_split, 1)
            for n, (w, parts) in enumerate(((wx_f, wx_p), (wh_f, wh_p))):
                dve.wait_ge(weights0_high, n + 1)
                nc.vector.tensor_tensor(parts[:, 1, :, cols], w[:, :, cols], parts[:, 0, :, cols],
                                        ALU.subtract).then_inc(weights0_split, 1)

            def reduce_crit(g, base, j, s):
                dve.wait_ge(crit_done[g], base + (j - crit_start(g) + 1))
                c = crit_columns(g, s)
                z = ps[:, c:c + CRIT_STEP].rearrange("p (m q b) -> p m b q", q=2, b=B)
                nc.vector.tensor_reduce(zc_view(g, s).rearrange("p (m b) -> p m b", b=B), z, AX.X, ALU.add)\
                    .then_inc(zc_ready[g], 1)

            def parts_sum(dst, c, ready):
                z = ps[:, c:c + REST_STEP].rearrange("p (m q b) -> p m b q", q=2, b=B)
                nc.vector.tensor_reduce(dst.rearrange("p (m b) -> p m b", b=B), z, AX.X, ALU.add)\
                    .then_inc(ready, 1)

            def reduce_o(g, base, j, s):
                dve.wait_ge(o_done[g], base + (j - crit_start(g) + 1))
                parts_sum(zo[g][:, :], o_columns(g, s), zo_ready[g])

            def reduce_rnn(g, base, j, s):
                dve.wait_ge(rnn_done[g], base + (j - rest_start(g) + 1))
                parts_sum(zr[g][:, :], r_columns(g, s), zr_ready[g])

            def products(g, base, j):
                dve.wait_ge(gates_ready[g], base + (j - crit_start(g) + 1))
                nc.vector.scalar_tensor_tensor(prod[g][:, :], gates[g][:, 0:8], 1.0, gates[g][:, 8:16],
                                               ALU.add, ALU.mult).then_inc(prod_ready[g], 1)

            def cell(g, base, j):
                dve.wait_ge(prod_ready[g], base + (j - crit_start(g) + 1))
                nc.vector.scalar_tensor_tensor(gates[g][:, 12:16], prod[g][:, 4:8], 0.5, prod[g][:, 0:4],
                                               ALU.mult, ALU.add).then_inc(cell_ready[g], 1)

            def h_views(g, s, rnn, lstm):
                lay = slice(0 if rnn else 1, 2 if lstm else 1)
                n = KT * B
                a, z = lay.start * n, lay.stop * n
                ins = (mult[g][:, a:z].rearrange("p (l k b) -> p l k b", k=KT, b=B),
                       rest[g][:, 4 + a:4 + z].rearrange("p (l k b) -> p l k b", k=KT, b=B))
                return ins, hist[g][:, lay, s % BODY, :, :], h_p[g][:, lay, :, 0, :], h_p[g][:, lay, :, 1, :]

            def hidden(g, base, j, s, rnn, lstm):
                for l in STREAMS[g]:
                    if works(l, s) and (s - LAG[l]) % CH == 0 and s - LAG[l] >= BODY:
                        dve.wait_ge(x_ready[l + 1], base + (j - LAG[l] - CH))
                if not lstm:
                    dve.wait_ge(tanh_r_ready[g], base + (j - rest_start(g) + 1))
                if lstm:
                    dve.wait_ge(tanh_c_ready[g], base + (j - crit_start(g) + 1))
                (m, t), hf, high, _ = h_views(g, s, rnn, lstm)
                nc.vector.tensor_tensor(high, m, t, ALU.mult)
                nc.vector.tensor_tensor(hf, m, t, ALU.mult).then_inc(hist_ready[g], 1)

            def hidden_low(g, base, j, s, rnn, lstm):
                dve.wait_ge(hist_ready[g], base + (j - rest_start(g) + 1))
                _, hf, high, low = h_views(g, s, rnn, lstm)
                nc.vector.tensor_tensor(low, hf, high, ALU.subtract).then_inc(h_ready[g], 1)

            def body(base, j, steady):
                s = time_of(base, j, steady)
                for g in range(2):
                    rnn, lstm = (works(l, s) for l in STREAMS[g])
                    back = 1 - g
                    other = [works(l, s - back) for l in STREAMS[1 - g]]
                    if lstm:
                        reduce_crit(g, base, j, s)
                    if any(other):
                        hidden_low(1 - g, base, j - back, s - back, *other)
                    if lstm:
                        reduce_o(g, base, j, s)
                    if rnn:
                        reduce_rnn(g, base, j, s)
                    if lstm:
                        products(g, base, j)
                        cell(g, base, j)
                    if rnn or lstm:
                        hidden(g, base, j, s, rnn, lstm)

            all_steps(dve, body, last=STEPS + 1)

        @block.tensor
        def _(pe):
            def weights(w, l, tile, kt):
                c = (TILE0[l] + tile) * P
                return w[:, kt, c:c + P]

            def recurrent(l, tiles, c, first, base, j, done):
                g, lay = l // 2, l % 2
                for m, tile in enumerate(tiles):
                    for kt in range(KT):
                        if first:
                            last = nc.tensor.matmul(ps[:, c + m * COLS:c + m * COLS + B],
                                                    weights(wh_f, l, tile, kt), cond_f[:, kt, :],
                                                    start=False, stop=True, skip_group_check=True)
                            continue
                        for part in range(2):
                            last = nc.tensor.matmul(ps[:, c + m * COLS:c + (m + 1) * COLS],
                                                    weights(wh_p[:, part], l, tile, kt),
                                                    h_p[g][:, lay, kt, :, :],
                                                    start=False, stop=True, skip_group_check=True)
                if done is not None:
                    last.then_inc(done, 1)

            def chunk_columns(l, tile, s):
                if not IS_LSTM[l]:
                    c, m, step = r_columns(l // 2, s), tile, REST_STEP
                elif tile in CRIT:
                    c, m, step = crit_columns(l // 2, s), CRIT.index(tile), CRIT_STEP
                else:
                    c, m, step = o_columns(l // 2, s), OGATE.index(tile), REST_STEP
                z = ps[:, c:c + CH * step].rearrange("p (t m q b) -> p m q t b", t=CH, q=2, b=B)
                return z[:, m]

            def bias_fill(layers, tiles, s):
                start = True
                for l in layers:
                    if works(l, s):
                        for tile in tiles:
                            nc.tensor.matmul(chunk_columns(l, tile, s)[:, 0], bias_p[:, :],
                                             patt[:, TILE0[l] + tile, :],
                                             start=start, stop=True, skip_group_check=True)
                            start = False

            def project(l, tile, kt, base, j, s, begins, ends):
                if begins:
                    pe.wait_ge(x_split[l], base + (j - LAG[l] + CH))
                p = (s - LAG[l]) // CH % 2
                for part in range(2):
                    mm = nc.tensor.matmul(chunk_columns(l, tile, s), weights(wx_p[:, part], l, tile, kt),
                                          x_p[l][:, p, kt, :, :].rearrange("p q c -> p (q c)"),
                                          start=False, stop=True, skip_group_check=True)
                if ends:
                    mm.then_inc(projected[l], CH)

            order = {True: CRIT + OGATE, False: RNN_TILES}

            def fill_jobs(phase):
                lstm = [(l, t, k) for l in (1, 3) for t in order[True] for k in range(KT)]
                rnn = [(l, t, k) for l in (0, 2) for t in order[False] for k in range(KT)]
                if 1 <= phase <= 11:
                    return lstm[3 * (phase - 1):3 * phase]
                if phase >= 12:
                    return {12: rnn[0:3], 13: rnn[3:5], 14: rnn[5:6], 15: rnn[6:8]}[phase]
                return []

            bias_jobs = {0: ((0, 2), RNN_TILES, CH), 
                         13: ((1,), CRIT, LSTM_PHASE + CH - 13), 14: ((3,), CRIT, LSTM_PHASE + CH - 14),
                         15: ((1, 3), OGATE, LSTM_PHASE + CH - 15)}

            def fill(base, j, s, steady, half):
                phase = s % CH
                if half == 0 and phase in bias_jobs:
                    layers, tiles, at = bias_jobs[phase]
                    if phase == 0 and works(2, s - 1) and works(2, s + at):
                        pe.wait_ge(zr_ready[1], base + (j - rest_start(1)))
                    bias_fill(layers, tiles, s + at)
                jobs = fill_jobs(phase)
                for l, tile, kt in (jobs[1:] if half else jobs[:1]):
                    at = (LSTM_PHASE if IS_LSTM[l] else CH) - phase
                    start = s + at
                    if not works(l, start):
                        continue
                    tiles = order[IS_LSTM[l]]
                    if start == LAG[l] and l and (tile, kt) == (tiles[0], 0):
                        pe.wait_ge(weights_split, 2 * l)
                    project(l, tile, kt, base, j + at, start, (tile, kt) == (tiles[0], 0),
                            (tile, kt) == (tiles[-1], KT - 1))

            pe.wait_ge(bias_split, 1)
            bias_fill((0,), RNN_TILES, 0)
            pe.wait_ge(weights0_split, 2)
            for tile in RNN_TILES:
                for kt in range(KT):
                    project(0, tile, kt, 0, 0, 0, (tile, kt) == (0, 0), (tile, kt) == (RNN_TILES[-1], KT - 1))

            def body(base, j, steady):
                s = time_of(base, j, steady)
                for g in range(2):
                    rnn_l, lstm_l = STREAMS[g]
                    rnn, lstm = works(rnn_l, s), works(lstm_l, s)
                    if (rnn or lstm) and (steady or s > rest_start(g)):
                        pe.wait_ge(h_ready[g], base + (j - rest_start(g)))
                    if lstm:
                        recurrent(lstm_l, CRIT, crit_columns(g, s), s == LAG[lstm_l], base, j, crit_done[g])
                    other, back = 1 - g, 1 - g
                    if lstm and works(STREAMS[other][1], s - back):
                        pe.wait_ge(zo_ready[other], base + (j - back - crit_start(other) + 1))
                    if lstm:
                        recurrent(lstm_l, OGATE, o_columns(g, s), s == LAG[lstm_l], base, j, o_done[g])
                    if rnn and works(STREAMS[other][0], s - back):
                        pe.wait_ge(zr_ready[other], base + (j - back - rest_start(other) + 1))
                    if rnn:
                        recurrent(rnn_l, RNN_TILES, r_columns(g, s), s == LAG[rnn_l], base, j, rnn_done[g])
                    fill(base, j, s, steady, g)

            all_steps(pe, body)


def kernel(x, cond_1024, L0_cond_Wx, L0_cond_Wh, L0_cond_b, L1_cond_Wx, L1_cond_Wh, L1_cond_b,
           L2_cond_Wx, L2_cond_Wh, L2_cond_b, L3_cond_Wx, L3_cond_Wh, L3_cond_b):
    import ml_dtypes
    import concourse.bacc as bacc
    from concourse.bass_utils import run_bass_kernel_spmd

    nc = bacc.Bacc("TRN2", target_bir_lowering=False, num_devices=1)
    xt = np.asarray(x).reshape(B, NCH, CH, KT, P).transpose(4, 1, 3, 2, 0).reshape(P, -1)
    arrays = {
        "x": xt,
        "cond": np.asarray(cond_1024).reshape(B, KT, P).transpose(2, 1, 0),
        "Wx0": L0_cond_Wx, "Wx1": L1_cond_Wx, "Wx2": L2_cond_Wx, "Wx3": L3_cond_Wx,
        "Wh0": L0_cond_Wh, "Wh1": L1_cond_Wh, "Wh2": L2_cond_Wh, "Wh3": L3_cond_Wh,
        "b0": L0_cond_b, "b1": L1_cond_b, "b2": L2_cond_b, "b3": L3_cond_b,
        "pattern": bias_patterns().astype(ml_dtypes.bfloat16),
    }
    half = np.ones((3, 32, 1), np.float32)
    for l in range(NL):
        if IS_LSTM[l]:
            half[:, TILE0[l]:TILE0[l] + SIGMOID_COLS // P] = 0.5
    arrays["half"] = half.reshape(96, 1)
    arrays = {k: np.ascontiguousarray(v) for k, v in arrays.items()}
    ap = {k: nc.dram_tensor(k, v.shape, mybir.dt.from_np(v.dtype), kind="ExternalInput").ap()
          for k, v in arrays.items()}
    out = nc.dram_tensor("out", (P, T * KT * B), F32, kind="ExternalOutput").ap()
    build(nc, ap["x"], ap["cond"], [ap[f"Wx{l}"] for l in range(NL)], [ap[f"Wh{l}"] for l in range(NL)],
          [ap[f"b{l}"] for l in range(NL)], ap["pattern"], ap["half"], out)
    r = run_bass_kernel_spmd(nc, [arrays], core_ids=[0])
    y = np.asarray(r.results[0]["out"]).reshape(P, NCH, KT, CH, B)
    return np.ascontiguousarray(y.transpose(4, 1, 3, 2, 0).reshape(B, T, D))
```

```python
from contextlib import ExitStack

import numpy as np

import concourse.bass as bass
from concourse import mybir

F32 = mybir.dt.float32
F16 = mybir.dt.float16
BF16 = mybir.dt.bfloat16
I32 = mybir.dt.int32
ALU = mybir.AluOpType
TANH = mybir.ActivationFunctionType.Tanh
COPY = mybir.ActivationFunctionType.Copy
AX = mybir.AxisListType

P = 128
B, T, D = 2, 1024, 256
KT = D // P
CH = 8
NCH = T // CH
RING = 2 * CH
BODY = 4 * RING
NL = 4
IS_LSTM = [False, True, False, True]
LAG = [0, 14, 24, 38]
RNN_PHASE = LAG[0] % CH
LSTM_PHASE = LAG[1] % CH
STREAMS = [(0, 1), (2, 3)]
STEPS = LAG[3] + T
LOOP_FROM = BODY
LOOP_TO = T - BODY

HSCALE = 2.0 ** 14
TOP = 2.0 ** 14
LEAST_MAX = 2.0 ** -20
EXPONENT_BITS = 0x7F800000

GATES = [4 * KT if lstm else KT for lstm in IS_LSTM]
TILE0 = [0, GATES[0], GATES[0] + GATES[1], GATES[0] + GATES[1] + GATES[2]]
NT = sum(GATES)
CRIT = [0, 1, 2, 3, 6, 7]
OGATE = [4, 5]
RNN_TILES = [0, 1]
ORDER = [CRIT + OGATE if lstm else RNN_TILES for lstm in IS_LSTM]
SIGMOIDS = 3

GROUPS = [(0,), (1,), (2, 3)]
WX, WH = 0, 1
PIECES = [[(l, w, gate) for l in group for w in (WX, WH) for gate in range(GATES[l] // KT)] for group in GROUPS]
PIECES_BEFORE = [0, len(PIECES[0]), len(PIECES[0]) + len(PIECES[1])]
GROUP_OF = [0, 1, 2, 2]
PIECES_FOR = [sum((1 + IS_LSTM[k] * 3) * 2 for k in range(l + 1)) for l in range(NL)]
FIND_AT = [None, 0, 10]
SCALE_AT = [None, 3, 16]
SPLIT_AT = [None, 4, 17]
SPLITS = [None, 2, 1]
XPARTS = 4

BANK = 512
COLS = 2 * B
CRIT_STEP = len(CRIT) * COLS
REST_STEP = KT * COLS
CRIT_BANK = [[0, 1], [2, 3]]
O_BANK = [4, 5]
R_BANK = [6, 7]
REST_REGION = CH * REST_STEP


def bias_patterns():
    out = np.zeros((3, 32, NT, CH * B), np.float32)
    for l in range(NL):
        for m, tile in enumerate(ORDER[l]):
            out[:, tile, TILE0[l] + m] = 1.0
    return out.reshape(96, -1)


def build(nc, x, cond, wx, wh, bias, pattern, half, out):
    ctx = ExitStack()
    with ctx:
        def sb(name, shape, dt=F32):
            return ctx.enter_context(nc.sbuf_tensor(name, shape, dt))

        def sem(name):
            return ctx.enter_context(nc.semaphore(name))

        w_f = [sb(f"w{n}_f", [P, KT, NT * P]) for n in "xh"]
        w_p = [sb(f"w{n}_p", [P, 2, KT, NT * P], F16) for n in "xh"]
        cond_f = sb("cond_f", [P, KT, B])
        cond_s = sb("cond_s", [P, NL, 2, KT, B])
        bias_f = sb("bias_f", [96, NL, P])
        bias_r = sb("bias_r", [96, 2, NL, P])
        bias_s = sb("bias_s", [96, 3, NL, P], BF16)
        bias_p = sb("bias_p", [96, NL, P], BF16)
        patt = sb("patt", [96, NT, CH * B], BF16)
        half_c = sb("half_c", [96, 2])
        largest = sb("largest", [P, XPARTS + NL * 2 * KT])
        largest_all = sb("largest_all", [P, XPARTS + NL * 2 * KT])
        x_most = sb("x_most", [P, 1])
        x_power = sb("x_power", [P, 1])
        x_inv = sb("x_inv", [P, 1])
        w_most = sb("w_most", [P, NL, 2])
        w_power = sb("w_power", [P, NL, 2])
        x_w = sb("x_w", [P, NL])
        total = sb("total", [P, NL])
        inv = sb("inv", [P, NL])
        w_scale = [sb(f"w{n}_scale", [P, 2, NL]) for n in "xh"]
        b_scale = sb("b_scale", [P, NL])
        z_scale = sb("z_scale", [P, NL])
        up = sb("up", [P, KT * CH * B])
        down = sb("down", [P, KT * CH * B])
        xsplit = sb("xsplit", [P, KT, CH * B])
        x_all = sb("x_all", [P, T * KT * B])
        xtmp = [sb(f"xtmp{l}", [P, KT, CH * B]) for l in range(NL)]
        x_p = [sb(f"x_p{l}", [P, 2, KT, 2, CH * B], F16) for l in range(NL)]
        xs = [sb(f"x{l}", [P, 2, KT, CH * B]) for l in range(NL + 1)]
        zo = [sb(f"zo{g}", [P, KT * B]) for g in range(2)]
        zr = [sb(f"zr{g}", [P, KT * B]) for g in range(2)]
        gates = [sb(f"gates{g}", [P, 16]) for g in range(2)]
        rest = [sb(f"rest{g}", [P, 12]) for g in range(2)]
        mult = [sb(f"mult{g}", [P, 8]) for g in range(2)]
        prod = [sb(f"prod{g}", [P, 8]) for g in range(2)]
        hist = [sb(f"hist{g}", [P, 2, RING, KT, B]) for g in range(2)]
        h_p = [sb(f"h_p{g}", [P, 2, KT, 2, B], F16) for g in range(2)]
        ps = ctx.enter_context(nc.psum_tensor("ps", [P, 8 * BANK], F32))

        w_loaded = [[sem(f"w{n}_loaded{l}") for n in "xh"] for l in range(NL)]
        x_loaded = [sem(f"x_loaded{i}") for i in range(XPARTS)]
        small_loaded = sem("small_loaded")
        consts_set = sem("consts_set")
        largest_found = sem("largest_found")
        largest_shared = sem("largest_shared")
        prep_chain = sem("prep_chain")
        pool_chain = sem("pool_chain")
        scales_set = sem("scales_set")
        weights_high = sem("weights_high")
        weights_split = sem("weights_split")
        bias_split = sem("bias_split")
        out_stored = sem("out_stored")
        x_ready = [sem(f"x_ready{l}") for l in range(NL + 1)]
        out_ready = sem("out_ready")
        x_tmp_ready = [sem(f"x_tmp_ready{l}") for l in range(NL)]
        x_split = [sem(f"x_split{l}") for l in range(NL)]
        projected = [sem(f"projected{l}") for l in range(NL)]
        crit_done = [sem(f"crit_done{g}") for g in range(2)]
        o_done = [sem(f"o_done{g}") for g in range(2)]
        rnn_done = [sem(f"rnn_done{g}") for g in range(2)]
        zc_ready = [sem(f"zc_ready{g}") for g in range(2)]
        zo_ready = [sem(f"zo_ready{g}") for g in range(2)]
        zr_ready = [sem(f"zr_ready{g}") for g in range(2)]
        gates_ready = [sem(f"gates_ready{g}") for g in range(2)]
        tanh_o_ready = [sem(f"tanh_o_ready{g}") for g in range(2)]
        tanh_r_ready = [sem(f"tanh_r_ready{g}") for g in range(2)]
        prod_ready = [sem(f"prod_ready{g}") for g in range(2)]
        cell_ready = [sem(f"cell_ready{g}") for g in range(2)]
        tanh_c_ready = [sem(f"tanh_c_ready{g}") for g in range(2)]
        hist_ready = [sem(f"hist_ready{g}") for g in range(2)]
        h_ready = [sem(f"h_ready{g}") for g in range(2)]

        block = ctx.enter_context(nc.Block())

        def works(layer, s):
            return LAG[layer] <= s < LAG[layer] + T

        def rest_start(g):
            return LAG[STREAMS[g][0]]

        def crit_start(g):
            return LAG[STREAMS[g][1]]

        def all_steps(eng, body, last=STEPS):
            for s in range(LOOP_FROM):
                body(0, s, False)
            with eng.Fori(LOOP_FROM, LOOP_TO - BODY + 1, BODY) as base:
                for j in range(BODY):
                    body(base, j, True)
            for s in range(LOOP_TO, last):
                body(0, s, False)

        def time_of(base, j, steady):
            return LOOP_FROM + j if steady else j

        def lstm_window(s):
            return (s - LSTM_PHASE) // CH

        def crit_columns(g, s):
            w = lstm_window(s)
            return CRIT_BANK[g][w % 2] * BANK + (s - LSTM_PHASE) % CH * CRIT_STEP

        def o_columns(g, s):
            w = lstm_window(s)
            return O_BANK[w % 2] * BANK + g * REST_REGION + (s - LSTM_PHASE) % CH * REST_STEP

        def r_columns(g, s):
            return R_BANK[s // CH % 2] * BANK + g * REST_REGION + s % CH * REST_STEP

        def zc_view(g, s):
            c = CRIT_BANK[g][lstm_window(s) % 2] * BANK + CH * CRIT_STEP
            return ps[:, c:c + len(CRIT) * B]

        def cell_view(g, s):
            c = CRIT_BANK[g][lstm_window(s) % 2] * BANK + CH * CRIT_STEP + len(CRIT) * B
            return ps[:, c:c + KT * B]

        def piece(l, gate):
            c = (TILE0[l] + gate * KT) * P
            return (lambda w: w[:, :, c:c + KT * P]), int(IS_LSTM[l] and gate < SIGMOIDS)

        def pieces_at(s):
            for group in (1, 2):
                a = (s - SPLIT_AT[group]) * SPLITS[group]
                if 0 <= a < len(PIECES[group]):
                    return [(PIECES_BEFORE[group] + a + n, PIECES[group][a + n]) for n in range(SPLITS[group])]
            return []

        def split_biases(group, engine, queue, link):
            a, z = GROUPS[group][0], GROUPS[group][-1] + 1
            r = [bias_r[:, 0, a:z, :], bias_r[:, 1, a:z, :]]
            for l in GROUPS[group]:
                link(engine.tensor_scalar(bias_r[:, 0, l, :], bias_f[:, l, :], b_scale[0:96, l:l + 1],
                                          half_c[:, IS_LSTM[l]:IS_LSTM[l] + 1], ALU.mult, ALU.mult))
            for q in range(3):
                link(engine.tensor_copy(bias_s[:, q, a:z, :], r[q % 2]))
                if q < 2:
                    link(engine.tensor_tensor(r[1 - q % 2], r[q % 2], bias_s[:, q, a:z, :], ALU.subtract))
            for q in range(3):
                rows = slice(32 * q, 32 * q + 32)
                engine.tensor_copy(bias_p[rows, a:z, :], bias_s[rows, q, a:z, :]).then_inc(bias_split, 1)
                queue.wait_ge(bias_split, 3 * group + q + 1)

        @block.sync
        def _(sp):
            def load(l, w):
                c, z = TILE0[l] * P, (TILE0[l] + GATES[l]) * P
                sp.dma_start(w_f[w][:, :, c:z], (wx, wh)[w][l].rearrange("(k p) n -> p k n", p=P))\
                    .then_inc(w_loaded[l][w], 16)

            load(0, WX)
            load(0, WH)
            n = T * KT * B // XPARTS
            for i in range(XPARTS):
                sp.dma_start(x_all[:, i * n:(i + 1) * n], x[:, i * n:(i + 1) * n]).then_inc(x_loaded[i], 16)
            for l in range(1, NL):
                load(l, WX)
                load(l, WH)

            def body(base, j, steady):
                s = time_of(base, j, steady)
                if (s - 1 - LAG[3]) % BODY == 0 and s - 1 - LAG[3] >= BODY:
                    t = j - 1 - LAG[3]
                    sp.wait_ge(out_ready, base + t)
                    at = bass.ds((base + (t - BODY)) * (KT * B), BODY * KT * B)
                    sp.dma_start(out[:, at], x_all[:, at]).then_inc(out_stored, 16)

            all_steps(sp, body, last=STEPS + 2)
            sp.wait_ge(out_stored, 16 * (T // BODY))

        @block.gpsimd
        def _(pool):
            nc.gpsimd.memset(up[:, :], HSCALE).then_inc(consts_set, 1)
            nc.gpsimd.memset(down[:, :], 1.0 / HSCALE).then_inc(consts_set, 1)
            pool.wait_ge(consts_set, 2)

            def largest_columns(group):
                c = XPARTS + GROUPS[group][0] * 2 * KT if group else 0
                return slice(c, XPARTS + (GROUPS[group][-1] + 1) * 2 * KT)

            def share_largest(group):
                cols = largest_columns(group)
                pool.wait_ge(largest_found, group + 1)
                nc.gpsimd.partition_all_reduce(largest_all[:, cols], largest[:, cols], P,
                                               bass.bass_isa.ReduceOp.max).then_inc(largest_shared, 1)

            chain = [0]

            def link(ins):
                chain[0] += 1
                ins.then_inc(pool_chain, 1)
                pool.wait_ge(pool_chain, chain[0])

            def flat(a, l, p):
                return a[l][:, p, :, :].rearrange("p k c -> p (k c)")

            def split_x(l, base, done, s_done):
                p = (s_done // CH - 1) % 2
                if s_done > CH:
                    pool.wait_ge(x_split[l], base + (done - CH))
                if s_done > RING:
                    pool.wait_ge(projected[l], base + (done - RING))
                pool.wait_ge(x_ready[l], base + done)
                nc.gpsimd.tensor_tensor(x_p[l][:, p, :, 0, :], xs[l][:, p, :, :], xsplit[:, :, :], ALU.mult)
                nc.gpsimd.tensor_tensor(xtmp[l][:, :, :], xs[l][:, p, :, :], xsplit[:, :, :], ALU.mult)\
                    .then_inc(x_tmp_ready[l], CH)
                pool.wait_ge(x_tmp_ready[l], base + done)
                nc.gpsimd.tensor_tensor(x_p[l][:, p, :, 1, :], xtmp[l][:, :, :], x_p[l][:, p, :, 0, :],
                                        ALU.subtract).then_inc(x_split[l], CH)

            def take_x(base, j, s):
                p = s // CH % 2
                if s >= RING:
                    pool.wait_ge(x_ready[1], base + (j - CH))
                    pool.wait_ge(x_split[0], base + (j - CH))
                nc.gpsimd.tensor_tensor(flat(xs, 0, p), x_all[:, bass.ds((base + j) * (KT * B), CH * KT * B)],
                                        up[:, :], ALU.mult).then_inc(x_ready[0], CH)
                split_x(0, base, j + CH, s + CH)

            def residual(l, base, j, s):
                g = l // 2
                p = (s - LAG[l] - CH) // CH % 2
                done = j - LAG[l]
                pool.wait_ge(hist_ready[g], base + (j - rest_start(g)))
                if l < NL - 1:
                    if s - LAG[l] > RING:
                        pool.wait_ge(x_ready[l + 2], base + (done - RING))
                        pool.wait_ge(x_split[l + 1], base + (done - RING))
                elif s - LAG[l] > RING:
                    pool.wait_ge(out_ready, base + (done - RING))
                slot = (s - CH) % RING
                first = min(CH, RING - slot)
                dst = xs[l + 1][:, p, :, :].rearrange("p k (t b) -> p t k b", b=B)
                src = xs[l][:, p, :, :].rearrange("p k (t b) -> p t k b", b=B)
                for a, z in ((0, first), (first, CH)):
                    if a < z:
                        at = (slot + a) % RING
                        nc.gpsimd.tensor_tensor(dst[:, a:z], src[:, a:z],
                                                hist[g][:, l % 2, at:at + z - a, :, :], ALU.add)\
                            .then_inc(x_ready[l + 1], z - a)
                if l < NL - 1:
                    split_x(l + 1, base, done, s - LAG[l])
                if l == NL - 1:
                    pool.wait_ge(x_ready[NL], base + done)
                    nc.gpsimd.tensor_tensor(x_all[:, bass.ds((base + (done - CH)) * (KT * B), CH * KT * B)],
                                            flat(xs, NL, p), down[:, :], ALU.mult).then_inc(out_ready, CH)

            share_largest(0)
            pool.wait_ge(scales_set, 1)
            link(nc.gpsimd.tensor_scalar(xsplit[:, :, :].rearrange("p k c -> p (k c)"), up[:, :],
                                         x_inv[:, :], TOP / HSCALE ** 2, ALU.mult, ALU.mult))
            take_x(0, 0, 0)
            take_x(0, CH, CH)

            def body(base, j, steady):
                s = time_of(base, j, steady)
                if s % CH == RNN_PHASE:
                    for l in (0, 2):
                        if steady or LAG[l] + CH <= s <= LAG[l] + T:
                            residual(l, base, j, s)
                if s % CH == 2 and s >= CH and (steady or s - 2 + CH < T):
                    take_x(base, j - 2 + CH, s - 2 + CH)
                if s % CH == LSTM_PHASE:
                    for l in (1, 3):
                        if steady or LAG[l] + CH <= s <= LAG[l] + T:
                            residual(l, base, j, s)
                for group in (1, 2):
                    if s == SCALE_AT[group] - 1:
                        share_largest(group)
                    if s == SCALE_AT[group]:
                        pool.wait_ge(scales_set, group + 1)
                        split_biases(group, nc.gpsimd, pool, link)

            all_steps(pool, body, last=STEPS + 1)

        @block.scalar
        def _(act):
            act.dma_start(cond_f[:, :, :], cond).then_inc(small_loaded, 16)
            act.dma_start(patt[:, :, :], pattern.rearrange("p (m c) -> p m c", m=NT)).then_inc(small_loaded, 16)
            act.dma_start(half_c[:, :], half).then_inc(small_loaded, 16)
            act.dma_start(bias_f[:, :, :], bias.rearrange("p (l n) -> p l n", n=P)).then_inc(small_loaded, 16)
            act.preload_act_table(TANH)
            z_factor = [act.alloc_register(f"z_factor{l}") for l in range(NL)]

            def take_scales(group):
                act.wait_ge(scales_set, group + 1)
                for l in GROUPS[group]:
                    act.reg_load(z_factor[l], z_scale[0:1, l:l + 1].bitcast(I32))

            def high_part(l, w, gate):
                view, factor = piece(l, gate)
                nc.scalar.activation(view(w_p[w][:, 0]), view(w_f[w]), COPY, scale=w_scale[w][:, factor, l:l + 1])\
                    .then_inc(weights_high, 1)

            take_scales(0)
            for which in PIECES[0]:
                high_part(*which)

            def body(base, j, steady):
                s = time_of(base, j, steady)
                for g in range(2):
                    rnn, lstm = (works(l, s) for l in STREAMS[g])
                    if lstm:
                        act.wait_ge(zc_ready[g], base + (j - crit_start(g) + 1))
                        nc.scalar.activation(gates[g][:, 0:12], zc_view(g, s), TANH, scale=z_factor[STREAMS[g][1]])\
                            .then_inc(gates_ready[g], 1)
                        act.wait_ge(zo_ready[g], base + (j - crit_start(g) + 1))
                        nc.scalar.activation(rest[g][:, 0:4], zo[g][:, :], TANH, scale=z_factor[STREAMS[g][1]])\
                            .then_inc(tanh_o_ready[g], 1)
                        act.wait_ge(tanh_o_ready[g], base + (j - crit_start(g) + 1))
                        nc.scalar.activation(mult[g][:, 4:8], rest[g][:, 0:4], COPY,
                                             bias=0.5 * HSCALE, scale=0.5 * HSCALE)
                    if rnn:
                        act.wait_ge(zr_ready[g], base + (j - rest_start(g) + 1))
                        nc.scalar.activation(rest[g][:, 4:8], zr[g][:, :], TANH, scale=z_factor[STREAMS[g][0]])\
                            .then_inc(tanh_r_ready[g], 1)
                    if lstm:
                        act.wait_ge(cell_ready[g], base + (j - crit_start(g) + 1))
                        nc.scalar.activation(rest[g][:, 8:12], cell_view(g, s), TANH, scale=0.5)\
                            .then_inc(tanh_c_ready[g], 1)
                if s in SPLIT_AT:
                    take_scales(SPLIT_AT.index(s))
                for _, which in pieces_at(s):
                    high_part(*which)

            all_steps(act, body)

        @block.vector
        def _(dve):
            for g in range(2):
                nc.vector.memset(gates[g][:, 12:16], 0.0)
                nc.vector.memset(mult[g][:, 0:4], HSCALE)
            chain = [0]

            def link(ins):
                chain[0] += 1
                ins.then_inc(prep_chain, 1)
                dve.wait_ge(prep_chain, chain[0])

            def find_largest(l, w, kt):
                c = XPARTS + (l * 2 + w) * KT + kt
                dve.wait_ge(w_loaded[l][w], 16)
                return nc.vector.tensor_reduce(largest[:, c:c + 1],
                                               w_f[w][:, kt, TILE0[l] * P:(TILE0[l] + GATES[l]) * P],
                                               AX.X, ALU.max, apply_absolute_value=True)

            def scales(group):
                a, z = GROUPS[group][0], GROUPS[group][-1] + 1
                dve.wait_ge(largest_shared, group + 1)
                if group == 0:
                    link(nc.vector.tensor_reduce(x_most[:, :], largest_all[:, 0:XPARTS], AX.X, ALU.max))
                    link(nc.vector.tensor_scalar(x_most[:, :], x_most[:, :], float(NL - 1), None, ALU.add))
                    link(nc.vector.tensor_scalar(x_power[:, :].bitcast(I32), x_most[:, :].bitcast(I32),
                                                 EXPONENT_BITS, None, ALU.bitwise_and))
                    link(nc.vector.reciprocal(x_inv[:, :], x_power[:, :]))
                found = largest_all[:, XPARTS + a * 2 * KT:XPARTS + z * 2 * KT]
                link(nc.vector.tensor_reduce(w_most[:, a:z, :],
                                             found.rearrange("p (l w k) -> p l w k", w=2, k=KT), AX.X, ALU.max))
                link(nc.vector.tensor_scalar(w_power[:, a:z, :].bitcast(I32), w_most[:, a:z, :].bitcast(I32),
                                             EXPONENT_BITS, None, ALU.bitwise_and))
                link(nc.vector.tensor_scalar(x_w[:, a:z], w_power[:, a:z, WX], x_power[:, :], None, ALU.mult))
                link(nc.vector.scalar_tensor_tensor(total[:, a:z], w_power[:, a:z, WH], LEAST_MAX, x_w[:, a:z],
                                                    ALU.max, ALU.max))
                link(nc.vector.reciprocal(inv[:, a:z], total[:, a:z]))
                nc.vector.tensor_scalar(b_scale[:, a:z], inv[:, a:z], TOP * HSCALE, None, ALU.mult)
                nc.vector.tensor_scalar(z_scale[:, a:z], total[:, a:z], 1.0 / (TOP * HSCALE), None, ALU.mult)
                for n, f in enumerate((1.0, 0.5)):
                    nc.vector.tensor_scalar(w_scale[WX][:, n, a:z], inv[:, a:z], x_power[:, :], HSCALE * f,
                                            ALU.mult, ALU.mult)
                    last = nc.vector.tensor_scalar(w_scale[WH][:, n, a:z], inv[:, a:z], TOP * f, None, ALU.mult)
                last.then_inc(scales_set, 1)

            def scaled_cond(group):
                dve.wait_ge(scales_set, group + 1)
                for l in GROUPS[group]:
                    for n in range(2):
                        nc.vector.tensor_scalar(cond_s[:, l, n], cond_f[:, :, :], w_scale[WH][:, n, l:l + 1],
                                                HSCALE, ALU.mult, ALU.mult)

            def low_part(number, l, w, gate):
                view, factor = piece(l, gate)
                dve.wait_ge(weights_high, number + 1)
                nc.vector.scalar_tensor_tensor(view(w_p[w][:, 1]), view(w_f[w]), w_scale[w][:, factor, l:l + 1],
                                               view(w_p[w][:, 0]), ALU.mult, ALU.subtract)\
                    .then_inc(weights_split, 1)

            for w in (WX, WH):
                for kt in range(KT):
                    find_largest(0, w, kt)
            for i in range(XPARTS):
                n = T * KT * B // XPARTS
                dve.wait_ge(x_loaded[i], 16)
                last = nc.vector.tensor_reduce(largest[:, i:i + 1], x_all[:, i * n:(i + 1) * n], AX.X, ALU.max,
                                               apply_absolute_value=True)
            last.then_inc(largest_found, 1)
            scales(0)
            dve.wait_ge(small_loaded, 16 * 4)
            scaled_cond(0)
            split_biases(0, nc.vector, dve, link)
            for number, which in enumerate(PIECES[0]):
                low_part(number, *which)

            def reduce_crit(g, base, j, s):
                dve.wait_ge(crit_done[g], base + (j - crit_start(g) + 1))
                c = crit_columns(g, s)
                z = ps[:, c:c + CRIT_STEP].rearrange("p (m q b) -> p m b q", q=2, b=B)
                nc.vector.tensor_reduce(zc_view(g, s).rearrange("p (m b) -> p m b", b=B), z, AX.X, ALU.add)\
                    .then_inc(zc_ready[g], 1)

            def parts_sum(dst, c, ready):
                z = ps[:, c:c + REST_STEP].rearrange("p (m q b) -> p m b q", q=2, b=B)
                nc.vector.tensor_reduce(dst.rearrange("p (m b) -> p m b", b=B), z, AX.X, ALU.add)\
                    .then_inc(ready, 1)

            def reduce_o(g, base, j, s):
                dve.wait_ge(o_done[g], base + (j - crit_start(g) + 1))
                parts_sum(zo[g][:, :], o_columns(g, s), zo_ready[g])

            def reduce_rnn(g, base, j, s):
                dve.wait_ge(rnn_done[g], base + (j - rest_start(g) + 1))
                parts_sum(zr[g][:, :], r_columns(g, s), zr_ready[g])

            def products(g, base, j):
                dve.wait_ge(gates_ready[g], base + (j - crit_start(g) + 1))
                nc.vector.scalar_tensor_tensor(prod[g][:, :], gates[g][:, 0:8], 1.0, gates[g][:, 8:16],
                                               ALU.add, ALU.mult).then_inc(prod_ready[g], 1)

            def cell(g, base, j, s):
                dve.wait_ge(prod_ready[g], base + (j - crit_start(g) + 1))
                nc.vector.scalar_tensor_tensor(cell_view(g, s), prod[g][:, 4:8], 0.5, prod[g][:, 0:4],
                                               ALU.mult, ALU.add).then_inc(cell_ready[g], 1)
                nc.vector.scalar_tensor_tensor(gates[g][:, 12:16], prod[g][:, 4:8], 0.5, prod[g][:, 0:4],
                                               ALU.mult, ALU.add)

            def h_views(g, s, rnn, lstm):
                lay = slice(0 if rnn else 1, 2 if lstm else 1)
                n = KT * B
                a, z = lay.start * n, lay.stop * n
                ins = (mult[g][:, a:z].rearrange("p (l k b) -> p l k b", k=KT, b=B),
                       rest[g][:, 4 + a:4 + z].rearrange("p (l k b) -> p l k b", k=KT, b=B))
                return ins, hist[g][:, lay, s % RING, :, :], h_p[g][:, lay, :, 0, :], h_p[g][:, lay, :, 1, :]

            def hidden(g, base, j, s, rnn, lstm):
                for l in STREAMS[g]:
                    if s >= T and works(l, s) and (s - LAG[l]) % CH == 0 and s - LAG[l] >= RING:
                        dve.wait_ge(x_ready[l + 1], base + (j - LAG[l] - CH))
                if not lstm:
                    dve.wait_ge(tanh_r_ready[g], base + (j - rest_start(g) + 1))
                if lstm:
                    dve.wait_ge(tanh_c_ready[g], base + (j - crit_start(g) + 1))
                (m, t), hf, high, _ = h_views(g, s, rnn, lstm)
                nc.vector.tensor_tensor(high, m, t, ALU.mult)
                nc.vector.tensor_tensor(hf, m, t, ALU.mult).then_inc(hist_ready[g], 1)

            def hidden_low(g, base, j, s, rnn, lstm):
                dve.wait_ge(hist_ready[g], base + (j - rest_start(g) + 1))
                _, hf, high, low = h_views(g, s, rnn, lstm)
                nc.vector.tensor_tensor(low, hf, high, ALU.subtract).then_inc(h_ready[g], 1)

            def body(base, j, steady):
                s = time_of(base, j, steady)
                for g in range(2):
                    rnn, lstm = (works(l, s) for l in STREAMS[g])
                    back = 1 - g
                    other = [works(l, s - back) for l in STREAMS[1 - g]]
                    if lstm:
                        reduce_crit(g, base, j, s)
                    if any(other):
                        hidden_low(1 - g, base, j - back, s - back, *other)
                    if lstm:
                        reduce_o(g, base, j, s)
                        products(g, base, j)
                    if rnn:
                        reduce_rnn(g, base, j, s)
                    if lstm:
                        cell(g, base, j, s)
                    if rnn or lstm:
                        hidden(g, base, j, s, rnn, lstm)
                if s == FIND_AT[1]:
                    for kt in range(KT):
                        find_largest(1, WX, kt)
                if s == FIND_AT[1] + 1:
                    for kt in range(KT):
                        last = find_largest(1, WH, kt)
                    last.then_inc(largest_found, 1)
                if s == FIND_AT[2]:
                    for w in (WX, WH):
                        for kt in range(KT):
                            find_largest(2, w, kt)
                for w in (WX, WH):
                    for kt in range(KT):
                        if s == FIND_AT[2] + 1 + w * KT + kt:
                            last = find_largest(3, w, kt)
                            if w == WH and kt == KT - 1:
                                last.then_inc(largest_found, 1)
                for group in (1, 2):
                    if s == SCALE_AT[group]:
                        scales(group)
                        scaled_cond(group)
                for number, which in pieces_at(s - 1):
                    low_part(number, *which)

            all_steps(dve, body, last=STEPS + 1)

        @block.tensor
        def _(pe):
            def weights(w, l, tile, kt):
                c = (TILE0[l] + tile) * P
                return w[:, kt, c:c + P]

            def recurrent(l, tiles, c, done):
                g, lay = l // 2, l % 2
                for m, tile in enumerate(tiles):
                    for kt in range(KT):
                        for part in range(2):
                            last = nc.tensor.matmul(ps[:, c + m * COLS:c + (m + 1) * COLS],
                                                    weights(w_p[WH][:, part], l, tile, kt),
                                                    h_p[g][:, lay, kt, :, :],
                                                    start=False, stop=True, skip_group_check=True)
                last.then_inc(done, 1)

            def first_products(l, m):
                g, first = l // 2, LAG[l]
                if not IS_LSTM[l]:
                    c, done = r_columns(g, first), rnn_done[g]
                elif m < len(CRIT):
                    c, done = crit_columns(g, first) + m * COLS, crit_done[g]
                else:
                    c, done = o_columns(g, first), o_done[g]
                for n, tile in enumerate(ORDER[l][m:m + 2]):
                    for kt in range(KT):
                        last = nc.tensor.matmul(ps[:, c + n * COLS:c + n * COLS + B],
                                                weights(w_f[WH], l, tile, kt),
                                                cond_s[:, l, int(IS_LSTM[l] and tile < SIGMOIDS * KT), kt, :],
                                                start=False, stop=True, skip_group_check=True)
                if m + 2 in (len(CRIT), len(ORDER[l])):
                    last.then_inc(done, 1)

            def chunk_columns(l, first, count, s):
                if not IS_LSTM[l]:
                    c, step = r_columns(l // 2, s), REST_STEP
                elif first < len(CRIT):
                    c, step = crit_columns(l // 2, s), CRIT_STEP
                else:
                    c, step, first = o_columns(l // 2, s), REST_STEP, first - len(CRIT)
                z = ps[:, c:c + CH * step].rearrange("p (t m q b) -> p m q t b", t=CH, q=2, b=B)
                return z[:, first:first + count]

            def bias_fill(layers, first, count, s):
                start = True
                for l in layers:
                    if works(l, s):
                        at = TILE0[l] + first
                        if s == LAG[l] and l:
                            pe.wait_ge(bias_split, 3 * (GROUP_OF[l] + 1))
                        nc.tensor.matmul(chunk_columns(l, first, count, s)[:, :, 0], bias_p[:, l, :],
                                         patt[:, at:at + count, :].rearrange("p m (t b) -> p m t b", b=B),
                                         start=start, stop=True, skip_group_check=True)
                        start = False

            def project(l, m, kt, base, j, s):
                if (m, kt) == (0, 0):
                    pe.wait_ge(x_split[l], base + (j - LAG[l] + CH))
                p = (s - LAG[l]) // CH % 2
                for part in range(2):
                    mm = nc.tensor.matmul(chunk_columns(l, m, 1, s)[:, 0],
                                          weights(w_p[WX][:, part], l, ORDER[l][m], kt),
                                          x_p[l][:, p, kt, :, :].rearrange("p q c -> p (q c)"),
                                          start=False, stop=True, skip_group_check=True)
                if (m, kt) == (len(ORDER[l]) - 1, KT - 1):
                    mm.then_inc(projected[l], CH)

            jobs_of = [[(l, m, kt) for m in range(len(ORDER[l])) for kt in range(KT)] for l in range(NL)]
            lstm_jobs = jobs_of[1] + jobs_of[3]
            fill_jobs = {(phase, half): [] for phase in range(CH) for half in range(2)}
            todo = list(lstm_jobs)
            for at in [(0, 1)] + [(phase, half) for phase in range(1, LSTM_PHASE) for half in range(2)]:
                count = 2 if at == (2, 1) else 3
                fill_jobs[at], todo = todo[:count], todo[count:]
            fill_jobs[LSTM_PHASE, 0], fill_jobs[LSTM_PHASE, 1] = jobs_of[0][:1], jobs_of[0][1:]
            fill_jobs[LSTM_PHASE + 1, 0], fill_jobs[LSTM_PHASE + 1, 1] = jobs_of[2][:2], jobs_of[2][2:]
            bias_jobs = {(0, 0): [((1,), 0, len(CRIT), LSTM_PHASE), ((3,), 0, len(CRIT), LSTM_PHASE)],
                         (2, 1): [((1, 3), len(CRIT), len(OGATE), LSTM_PHASE - 2)],
                         (LSTM_PHASE, 0): [((0, 2), 0, len(RNN_TILES), CH - LSTM_PHASE)]}

            def fill(base, j, s, half):
                phase = s % CH
                for layers, first, count, to in bias_jobs.get((phase, half), []):
                    bias_fill(layers, first, count, s + to)
                for l, m, kt in fill_jobs[phase, half]:
                    to = (LSTM_PHASE if IS_LSTM[l] else CH) - phase
                    start = s + to
                    if not works(l, start):
                        continue
                    if start == LAG[l] and l and (m, kt) == (0, 0):
                        pe.wait_ge(weights_split, PIECES_FOR[l])
                    project(l, m, kt, base, j + to, start)

            pe.wait_ge(bias_split, 3)
            bias_fill((0,), 0, len(RNN_TILES), 0)
            pe.wait_ge(weights_split, PIECES_FOR[0])
            for _, m, kt in jobs_of[0]:
                project(0, m, kt, 0, 0, 0)
            first_products(0, 0)

            def body(base, j, steady):
                s = time_of(base, j, steady)
                for g in range(2):
                    rnn_l, lstm_l = STREAMS[g]
                    rnn, lstm = works(rnn_l, s), works(lstm_l, s)
                    if (rnn or lstm) and (steady or s > rest_start(g)):
                        pe.wait_ge(h_ready[g], base + (j - rest_start(g)))
                    if lstm and s > LAG[lstm_l]:
                        recurrent(lstm_l, CRIT, crit_columns(g, s), crit_done[g])
                    other, back = 1 - g, 1 - g
                    if lstm and works(STREAMS[other][1], s - back):
                        pe.wait_ge(zo_ready[other], base + (j - back - crit_start(other) + 1))
                    if lstm and s > LAG[lstm_l]:
                        recurrent(lstm_l, OGATE, o_columns(g, s), o_done[g])
                    if rnn and works(STREAMS[other][0], s - back):
                        pe.wait_ge(zr_ready[other], base + (j - back - rest_start(other) + 1))
                    if rnn and s > LAG[rnn_l]:
                        recurrent(rnn_l, RNN_TILES, r_columns(g, s), rnn_done[g])
                    fill(base, j, s, g)
                for l in range(1, NL):
                    m = len(ORDER[l]) - 2 * (LAG[l] - s)
                    if 0 <= m < len(ORDER[l]):
                        if m == 0:
                            pe.wait_ge(weights_split, PIECES_FOR[l])
                        first_products(l, m)

            all_steps(pe, body)


def kernel(x, cond_1024, L0_cond_Wx, L0_cond_Wh, L0_cond_b, L1_cond_Wx, L1_cond_Wh, L1_cond_b,
           L2_cond_Wx, L2_cond_Wh, L2_cond_b, L3_cond_Wx, L3_cond_Wh, L3_cond_b):
    import ml_dtypes
    import concourse.bacc as bacc
    from concourse.bass_utils import run_bass_kernel_spmd

    nc = bacc.Bacc("TRN2", target_bir_lowering=False, num_devices=1)
    xt = np.asarray(x).reshape(B, NCH, CH, KT, P).transpose(4, 1, 3, 2, 0).reshape(P, -1)
    arrays = {
        "x": xt,
        "cond": np.asarray(cond_1024).reshape(B, KT, P).transpose(2, 1, 0),
        "Wx0": L0_cond_Wx, "Wx1": L1_cond_Wx, "Wx2": L2_cond_Wx, "Wx3": L3_cond_Wx,
        "Wh0": L0_cond_Wh, "Wh1": L1_cond_Wh, "Wh2": L2_cond_Wh, "Wh3": L3_cond_Wh,
        "biases": np.zeros((3, 32, NL, P), np.float32),
        "pattern": bias_patterns().astype(ml_dtypes.bfloat16),
    }
    for l, b in enumerate((L0_cond_b, L1_cond_b, L2_cond_b, L3_cond_b)):
        arrays["biases"][:, :GATES[l], l] = np.asarray(b).reshape(GATES[l], P)
    arrays["biases"] = arrays["biases"].reshape(96, NL * P)
    half = np.ones((3, 32, 2), np.float32)
    half[:, :SIGMOIDS * KT, 1] = 0.5
    arrays["half"] = half.reshape(96, 2)
    arrays = {k: np.ascontiguousarray(v) for k, v in arrays.items()}
    ap = {k: nc.dram_tensor(k, v.shape, mybir.dt.from_np(v.dtype), kind="ExternalInput").ap()
          for k, v in arrays.items()}
    out = nc.dram_tensor("out", (P, T * KT * B), F32, kind="ExternalOutput").ap()
    build(nc, ap["x"], ap["cond"], [ap[f"Wx{l}"] for l in range(NL)], [ap[f"Wh{l}"] for l in range(NL)],
          ap["biases"], ap["pattern"], ap["half"], out)
    r = run_bass_kernel_spmd(nc, [arrays], core_ids=[0])
    y = np.asarray(r.results[0]["out"]).reshape(P, NCH, KT, CH, B)
    return np.ascontiguousarray(y.transpose(4, 1, 3, 2, 0).reshape(B, T, D))
```
